# Optimizing a Trainium2 kernel written in Bass

```python
import numpy as np
import jax
import jax.numpy as jnp

def _softmax(x, axis=-1):
    return jax.nn.softmax(x, axis=axis)

def _gelu(x):
    return jax.nn.gelu(x, approximate=True)

def _silu(x):
    return jax.nn.silu(x)

def _sigmoid(x):
    return jax.nn.sigmoid(x)

def _layernorm(x, axis=-1, eps=1e-05):
    m = jnp.mean(x, axis=axis, keepdims=True)
    v = jnp.var(x, axis=axis, keepdims=True)
    return (x - m) / jnp.sqrt(v + eps)

def _scatter_add(tgt, idx, src, axis=0):
    return tgt.at[idx].add(src)

def _segment_sum(src, seg, n):
    return jax.ops.segment_sum(src, seg, n)
kernel_name = 'mk_decoder_preln_d2_seqx_r8_96b17c'

def setup_inputs(seed: int=0):
    np.random.seed(seed)
    _w = jnp.asarray

    def _rec_inputs():
        import jax
        import jax.numpy as jnp
        _rk = jax.random.key(seed)
        x = 7.22e-05 + 1 * jax.random.normal(jax.random.fold_in(_rk, 1), (4, 512, 128), jnp.float32)
        _lenS = 512 - jax.random.randint(jax.random.fold_in(_rk, 7), (4,), 0, max(1, 512 // 4) + 1, jnp.int32)
        _lenS2 = 32 - jax.random.randint(jax.random.fold_in(_rk, 8), (4,), 0, max(1, 32 // 4) + 1, jnp.int32)
        _ctx_1024P = jax.random.normal(jax.random.fold_in(_rk, 11), (4, 16, 128), jnp.float32)
        _ctx_1024c = jax.random.dirichlet(jax.random.fold_in(_rk, 511), 0.3 * jnp.ones((16,), jnp.float32), (4, 32))
        _ctx_1024t = jnp.einsum('bsk,bkd->bsd', _ctx_1024c, _ctx_1024P)
        _ctx_1024t = _ctx_1024t * jax.lax.rsqrt(jnp.mean(jnp.square(_ctx_1024t)) + 1e-12) * 0.953939
        ctx_1024 = 4.13588e-05 + 0.999923 * (_ctx_1024t + 0.3 * jax.random.normal(jax.random.fold_in(_rk, 611), (4, 32, 128), jnp.float32))
        _validS = jnp.arange(512)[None, :] < _lenS[:, None]
        _validS2 = jnp.arange(32)[None, :] < _lenS2[:, None]
        _causal = jnp.tril(jnp.ones((512, 512), dtype=bool))
        mask_1xSxS2_ff0 = jnp.where(jnp.ones((1, 512, 32), dtype=bool), 0.0, -1000000000.0).astype(jnp.float32)
        mask_BxS2_bf0 = jnp.logical_not(jnp.ones((4, 32), dtype=bool))
        return (x, ctx_1024, mask_1xSxS2_ff0, mask_BxS2_bf0)
    x, ctx_1024, mask_1xSxS2_ff0, mask_BxS2_bf0 = _rec_inputs()

    def _L0_attn_setup():
        import jax, jax.numpy as jnp
        import numpy as np
        HEADS = 16
        DIMS = [64, 64, 64, 64]
        EPS = 0.0001
        P_POW = 2

        def _cdist(Q, K):
            q2 = jnp.sum(Q * Q, axis=-1)
            k2 = jnp.sum(K * K, axis=-1)
            qk = jnp.einsum('hbtd,hbsd->hbts', Q, K)
            d2 = q2[..., :, None] + k2[..., None, :] - 2.0 * qk
            return jnp.sqrt(jnp.maximum(d2, 0.0))
        key = jax.random.key(seed)
        ks = jax.random.split(key, 4)
        b, t, d_in = (2, 256, 128)
        d_proj = HEADS * sum(DIMS)
        X = jax.random.normal(ks[0], (b, t, d_in), dtype=jnp.float32)
        W_in = jax.random.normal(ks[1], (d_in, d_proj), dtype=jnp.float32) * d_in ** (-0.5)
        b_in = jnp.zeros((d_proj,), dtype=jnp.float32)
        W_out = jax.random.normal(ks[2], (HEADS * DIMS[2], d_in), dtype=jnp.float32) * (HEADS * DIMS[2]) ** (-0.5)
        b_out = jnp.zeros((d_in,), dtype=jnp.float32)
        return {'X': X, 'W_in': W_in, 'b_in': b_in, 'W_out': W_out, 'b_out': b_out}
    _L0_attn_all = _L0_attn_setup()
    _L0_attn_in = {k: v for k, v in _L0_attn_all.items() if k in ('W_in', 'b_in', 'W_out', 'b_out')}
    del _L0_attn_all

    def _L0_xattn_setup():
        import jax, jax.numpy as jnp
        import numpy as np
        B, S, D_IN, D_MODEL = (4, 256, 128, 128)
        key = jax.random.key(seed)
        ks = jax.random.split(key, 8)
        glorot = np.sqrt(6.0 / (D_IN + D_MODEL))
        inp = {'q': jax.random.normal(ks[0], (B, S, D_IN), dtype=jnp.float32), 'k': jax.random.normal(ks[1], (B, S, D_IN), dtype=jnp.float32), 'v': jax.random.normal(ks[2], (B, S, D_IN), dtype=jnp.float32), 'mask': jnp.zeros((1, S, S), dtype=jnp.float32), 'kernel_q': jax.random.uniform(ks[3], (1, 1, D_IN, D_MODEL), jnp.float32, -glorot, glorot), 'kernel_k': jax.random.uniform(ks[4], (1, 1, D_IN, D_MODEL), jnp.float32, -glorot, glorot), 'kernel_v': jax.random.uniform(ks[5], (1, 1, D_IN, D_MODEL), jnp.float32, -glorot, glorot), 'bias_q': 0.05 * jax.random.normal(ks[6], (D_MODEL,), dtype=jnp.float32), 'bias_k': 0.05 * jax.random.normal(ks[7], (D_MODEL,), dtype=jnp.float32), 'bias_v': 0.05 * jax.random.normal(jax.random.fold_in(key, 7), (D_MODEL,), dtype=jnp.float32)}
        return inp
    _L0_xattn_all = _L0_xattn_setup()
    _L0_xattn_in = {k: v for k, v in _L0_xattn_all.items() if k in ('kernel_q', 'kernel_k', 'kernel_v', 'bias_q', 'bias_k', 'bias_v')}
    del _L0_xattn_all

    def _L0_ffn_setup():
        import jax, jax.numpy as jnp
        import numpy as np
        import math
        D = 128
        H = 16
        E = 8
        TOPK = 2
        LAT = D // 2
        KPH = LAT // H
        HD = D // H

        def _forward(hs, q_w, q_b, k_w, k_b, v_w, v_b, o_w, o_b, router_w, router_b, w1, b1, w2, b2):
            B, S, _ = hs.shape
            Q = (hs @ q_w + q_b).reshape(B, S, H, HD).transpose(0, 2, 1, 3)
            K = (hs @ k_w + k_b).reshape(B, S, H, KPH).transpose(0, 2, 1, 3)
            V = (hs @ v_w + v_b).reshape(B, S, H, KPH).transpose(0, 2, 1, 3)
            scores = jnp.einsum('bhsk,bhtk->bhst', Q[..., :KPH], K) / math.sqrt(KPH)
            attn = jax.nn.softmax(scores, axis=-1)
            ao = jnp.einsum('bhst,bhtv->bhsv', attn, V)
            ao = ao.transpose(0, 2, 1, 3).reshape(B, S, H * KPH)
            ao = jnp.concatenate([ao, jnp.zeros((B, S, D - LAT), ao.dtype)], axis=-1)
            mla_out = ao @ o_w + o_b
            probs = jax.nn.softmax(mla_out @ router_w + router_b, axis=-1)
            topw, topi = jax.lax.top_k(probs, TOPK)
            topw = topw / (topw.sum(-1, keepdims=True) + 1e-08)
            combine = jnp.sum(jax.nn.one_hot(topi, E, dtype=probs.dtype) * topw[..., None], axis=-2)
            h1 = jnp.einsum('bsd,edf->ebsf', mla_out, w1) + b1[:, None, None, :]
            h1 = jax.nn.gelu(h1, approximate=False)
            h2 = jnp.einsum('ebsf,efd->ebsd', h1, w2) + b2[:, None, None, :]
            moe_out = jnp.einsum('bse,ebsd->bsd', combine, h2)
            return hs + 0.3 * moe_out
        key = jax.random.key(seed)
        ks = jax.random.split(key, 16)
        s = 0.02
        inp = {'hidden_states': jax.random.normal(ks[0], (2, 256, D), jnp.float32), 'q_w': jax.random.normal(ks[1], (D, D), jnp.float32) * s, 'q_b': jnp.zeros((D,), jnp.float32), 'k_w': jax.random.normal(ks[2], (D, LAT), jnp.float32) * s, 'k_b': jnp.zeros((LAT,), jnp.float32), 'v_w': jax.random.normal(ks[3], (D, LAT), jnp.float32) * s, 'v_b': jnp.zeros((LAT,), jnp.float32), 'o_w': jax.random.normal(ks[4], (D, D), jnp.float32) * s, 'o_b': jnp.zeros((D,), jnp.float32), 'router_w': jax.random.normal(ks[5], (D, E), jnp.float32) * s, 'router_b': jnp.zeros((E,), jnp.float32), 'w1': jax.random.normal(ks[6], (E, D, 2 * D), jnp.float32) * s, 'b1': jnp.zeros((E, 2 * D), jnp.float32), 'w2': jax.random.normal(ks[7], (E, 2 * D, D), jnp.float32) * s, 'b2': jnp.zeros((E, D), jnp.float32)}
        return inp
    _L0_ffn_all = _L0_ffn_setup()
    _L0_ffn_in = {k: v for k, v in _L0_ffn_all.items() if k in ('q_w', 'q_b', 'k_w', 'k_b', 'v_w', 'v_b', 'o_w', 'o_b', 'router_w', 'router_b', 'w1', 'b1', 'w2', 'b2')}
    del _L0_ffn_all

    def _L1_attn_setup():
        import jax, jax.numpy as jnp
        import numpy as np
        import math
        B, T, DIM = (4, 256, 128)
        N_HEADS, HEAD_DIM = (8, 128)
        WINDOW = 16
        EPS = 1e-06
        NEG = -1000000000.0

        def _alibi_slopes(n_heads):
            r = 2.0 ** (-8.0 / n_heads)
            return jnp.asarray([r ** i for i in range(n_heads)], dtype=jnp.float32)

        def _rms_norm(x, w, eps):
            var = jnp.mean(jnp.square(x), axis=-1, keepdims=True)
            return x * jax.lax.rsqrt(var + eps) * w
        key = jax.random.key(seed)
        ks = jax.random.split(key, 7)
        s = 1.0 / math.sqrt(DIM)
        return {'x': jax.random.normal(ks[0], (B, T, DIM), dtype=jnp.float32), 'wq': jax.random.normal(ks[1], (DIM, N_HEADS * HEAD_DIM), dtype=jnp.float32) * s, 'wk': jax.random.normal(ks[2], (DIM, N_HEADS * HEAD_DIM), dtype=jnp.float32) * s, 'wv': jax.random.normal(ks[3], (DIM, N_HEADS * HEAD_DIM), dtype=jnp.float32) * s, 'wo': jax.random.normal(ks[4], (N_HEADS * HEAD_DIM, DIM), dtype=jnp.float32) * s, 'q_norm_w': jnp.ones((N_HEADS * HEAD_DIM,), dtype=jnp.float32), 'k_norm_w': jnp.ones((N_HEADS * HEAD_DIM,), dtype=jnp.float32)}
    _L1_attn_all = _L1_attn_setup()
    _L1_attn_in = {k: v for k, v in _L1_attn_all.items() if k in ('wq', 'wk', 'wv', 'wo', 'q_norm_w', 'k_norm_w')}
    del _L1_attn_all

    def _L1_xattn_setup():
        import jax, jax.numpy as jnp
        import numpy as np
        B, SQ, SKV, D, H = (2, 256, 256, 128, 16)
        HD = D // H

        def cross_attention(query, context, mask, Wq, bq, Wkv, bkv, Wout, bout, num_heads):
            b, sq, d = query.shape
            skv = context.shape[1]
            hd = d // num_heads
            scale = hd ** (-0.5)
            q = query @ Wq + bq
            kv = context @ Wkv + bkv
            kv = kv.reshape(b, skv, 2, num_heads, hd).transpose(2, 0, 3, 1, 4)
            k, v = (kv[0], kv[1])
            q = q.reshape(b, sq, num_heads, hd).transpose(0, 2, 1, 3)
            scores = jnp.einsum('bhid,bhjd->bhij', q, k) * scale
            scores = jnp.where(mask[:, None, None, :], -jnp.inf, scores)
            attn = jax.nn.softmax(scores, axis=-1)
            out = jnp.einsum('bhij,bhjd->bhid', attn, v)
            out = out.transpose(0, 2, 1, 3).reshape(b, sq, d)
            return out @ Wout + bout
        key = jax.random.key(seed)
        ks = jax.random.split(key, 6)
        scale = 1.0 / np.sqrt(D)
        return {'query': jax.random.normal(ks[0], (B, SQ, D), dtype=jnp.float32), 'context': jax.random.normal(ks[1], (B, SKV, D), dtype=jnp.float32), 'mask': jnp.zeros((B, SKV), dtype=bool), 'Wq': jax.random.normal(ks[2], (D, D), dtype=jnp.float32) * scale, 'bq': jnp.zeros((D,), dtype=jnp.float32), 'Wkv': jax.random.normal(ks[3], (D, 2 * D), dtype=jnp.float32) * scale, 'bkv': jnp.zeros((2 * D,), dtype=jnp.float32), 'Wout': jax.random.normal(ks[4], (D, D), dtype=jnp.float32) * scale, 'bout': jnp.zeros((D,), dtype=jnp.float32), 'num_heads': H}
    _L1_xattn_all = _L1_xattn_setup()
    _L1_xattn_in = {k: v for k, v in _L1_xattn_all.items() if k in ('Wq', 'bq', 'Wkv', 'bkv', 'Wout', 'bout')}
    del _L1_xattn_all

    def _L1_ffn_setup():
        import jax, jax.numpy as jnp
        import numpy as np
        BLOCK = 16
        _GRID = jnp.array([0.0, 0.5, 1.0, 1.5, 2.0, 3.0, 4.0, 6.0], dtype=jnp.float32)
        _MID = jnp.array([0.25, 0.75, 1.25, 1.75, 2.5, 3.5, 5.0], dtype=jnp.float32)

        def fp4_quant_dequant(x):
            shape = x.shape
            xb = x.reshape(shape[:-1] + (shape[-1] // BLOCK, BLOCK))
            scale = jnp.max(jnp.abs(xb), axis=-1, keepdims=True) / 6.0
            scale = jnp.maximum(scale, jnp.float32(1e-12))
            xn = xb / scale
            idx = jnp.searchsorted(_MID, jnp.abs(xn))
            q = _GRID[idx] * jnp.sign(xn) * scale
            return q.reshape(shape)

        def fp4_linear(x, w):
            xq = fp4_quant_dequant(x)
            wq = fp4_quant_dequant(w)
            return jnp.einsum('bsk,nk->bsn', xq, wq)
        key = jax.random.key(seed)
        k1, k2, k3, k4 = jax.random.split(key, 4)
        H, I = (128, 352)
        x = jax.random.normal(k1, (4, 512, H), dtype=jnp.float32)
        w_gate = jax.random.normal(k2, (I, H), dtype=jnp.float32) * 0.02
        w_up = jax.random.normal(k3, (I, H), dtype=jnp.float32) * 0.02
        w_down = jax.random.normal(k4, (H, I), dtype=jnp.float32) * 0.02
        return {'x': x, 'w_gate': w_gate, 'w_up': w_up, 'w_down': w_down}
    _L1_ffn_all = _L1_ffn_setup()
    _L1_ffn_in = {k: v for k, v in _L1_ffn_all.items() if k in ('w_gate', 'w_up', 'w_down')}
    del _L1_ffn_all
    return {'x': x, 'ctx_1024': ctx_1024, 'mask_1xSxS2_ff0': mask_1xSxS2_ff0, 'mask_BxS2_bf0': mask_BxS2_bf0, 'L0_attn_W_in': _L0_attn_in['W_in'], 'L0_attn_b_in': _L0_attn_in['b_in'], 'L0_attn_W_out': _L0_attn_in['W_out'], 'L0_attn_b_out': _L0_attn_in['b_out'], 'L0_xattn_kernel_q': _L0_xattn_in['kernel_q'], 'L0_xattn_kernel_k': _L0_xattn_in['kernel_k'], 'L0_xattn_kernel_v': _L0_xattn_in['kernel_v'], 'L0_xattn_bias_q': _L0_xattn_in['bias_q'], 'L0_xattn_bias_k': _L0_xattn_in['bias_k'], 'L0_xattn_bias_v': _L0_xattn_in['bias_v'], 'L0_ffn_q_w': _L0_ffn_in['q_w'], 'L0_ffn_q_b': _L0_ffn_in['q_b'], 'L0_ffn_k_w': _L0_ffn_in['k_w'], 'L0_ffn_k_b': _L0_ffn_in['k_b'], 'L0_ffn_v_w': _L0_ffn_in['v_w'], 'L0_ffn_v_b': _L0_ffn_in['v_b'], 'L0_ffn_o_w': _L0_ffn_in['o_w'], 'L0_ffn_o_b': _L0_ffn_in['o_b'], 'L0_ffn_router_w': _L0_ffn_in['router_w'], 'L0_ffn_router_b': _L0_ffn_in['router_b'], 'L0_ffn_w1': _L0_ffn_in['w1'], 'L0_ffn_b1': _L0_ffn_in['b1'], 'L0_ffn_w2': _L0_ffn_in['w2'], 'L0_ffn_b2': _L0_ffn_in['b2'], 'L1_attn_wq': _L1_attn_in['wq'], 'L1_attn_wk': _L1_attn_in['wk'], 'L1_attn_wv': _L1_attn_in['wv'], 'L1_attn_wo': _L1_attn_in['wo'], 'L1_attn_q_norm_w': _L1_attn_in['q_norm_w'], 'L1_attn_k_norm_w': _L1_attn_in['k_norm_w'], 'L1_xattn_Wq': _L1_xattn_in['Wq'], 'L1_xattn_bq': _L1_xattn_in['bq'], 'L1_xattn_Wkv': _L1_xattn_in['Wkv'], 'L1_xattn_bkv': _L1_xattn_in['bkv'], 'L1_xattn_Wout': _L1_xattn_in['Wout'], 'L1_xattn_bout': _L1_xattn_in['bout'], 'L1_ffn_w_gate': _L1_ffn_in['w_gate'], 'L1_ffn_w_up': _L1_ffn_in['w_up'], 'L1_ffn_w_down': _L1_ffn_in['w_down']}

def reference(x, ctx_1024, mask_1xSxS2_ff0, mask_BxS2_bf0, L0_attn_W_in, L0_attn_b_in, L0_attn_W_out, L0_attn_b_out, L0_xattn_kernel_q, L0_xattn_kernel_k, L0_xattn_kernel_v, L0_xattn_bias_q, L0_xattn_bias_k, L0_xattn_bias_v, L0_ffn_q_w, L0_ffn_q_b, L0_ffn_k_w, L0_ffn_k_b, L0_ffn_v_w, L0_ffn_v_b, L0_ffn_o_w, L0_ffn_o_b, L0_ffn_router_w, L0_ffn_router_b, L0_ffn_w1, L0_ffn_b1, L0_ffn_w2, L0_ffn_b2, L1_attn_wq, L1_attn_wk, L1_attn_wv, L1_attn_wo, L1_attn_q_norm_w, L1_attn_k_norm_w, L1_xattn_Wq, L1_xattn_bq, L1_xattn_Wkv, L1_xattn_bkv, L1_xattn_Wout, L1_xattn_bout, L1_ffn_w_gate, L1_ffn_w_up, L1_ffn_w_down):
    import jax
    import jax.numpy as jnp

    def _L0_attn_ref(X, W_in, b_in, W_out, b_out):
        import jax, jax.numpy as jnp
        import numpy as np
        HEADS = 16
        DIMS = [64, 64, 64, 64]
        EPS = 0.0001
        P_POW = 2

        def _cdist(Q, K):
            q2 = jnp.sum(Q * Q, axis=-1)
            k2 = jnp.sum(K * K, axis=-1)
            qk = jnp.einsum('hbtd,hbsd->hbts', Q, K)
            d2 = q2[..., :, None] + k2[..., None, :] - 2.0 * qk
            return jnp.sqrt(jnp.maximum(d2, 0.0))
        b, t, _ = X.shape
        P = X @ W_in + b_in
        P = P.reshape(b, t, HEADS, sum(DIMS))
        P = jnp.transpose(P, (2, 0, 1, 3))
        splits = np.cumsum(DIMS)[:-1]
        Q, K, V, G = jnp.split(P, splits, axis=-1)
        W = jnp.power(EPS + _cdist(Q, K), -P_POW)
        W = W / (EPS + jnp.sum(W, axis=-1, keepdims=True))
        A = jnp.einsum('hbts,hbse->hbte', W, V)
        H = G * A
        H = jnp.transpose(H, (1, 2, 0, 3)).reshape(b, t, HEADS * DIMS[2])
        return H @ W_out + b_out

    def _L0_xattn_ref(q, k, v, mask, kernel_q, kernel_k, kernel_v, bias_q, bias_k, bias_v):
        import jax, jax.numpy as jnp
        import numpy as np
        B, S, D_IN, D_MODEL = (4, 256, 128, 128)
        Wq, Wk, Wv = (kernel_q[0, 0], kernel_k[0, 0], kernel_v[0, 0])
        qp = jax.nn.relu(jnp.einsum('bsd,de->bse', q, Wq) + bias_q)
        kp = jax.nn.relu(jnp.einsum('bsd,de->bse', k, Wk) + bias_k)
        vp = jax.nn.relu(jnp.einsum('bsd,de->bse', v, Wv) + bias_v)
        scores = jax.nn.relu(jnp.einsum('bqe,bke->bqk', qp, kp))
        dk = jnp.asarray(kp.shape[-1], dtype=scores.dtype)
        logits = scores / jnp.sqrt(dk) + mask
        out = jax.nn.relu(jnp.einsum('bqk,bke->bqe', logits, vp))
        return out

    def _L0_ffn_ref(hidden_states, q_w, q_b, k_w, k_b, v_w, v_b, o_w, o_b, router_w, router_b, w1, b1, w2, b2):
        import jax, jax.numpy as jnp
        import numpy as np
        import math
        D = 128
        H = 16
        E = 8
        TOPK = 2
        LAT = D // 2
        KPH = LAT // H
        HD = D // H

        def _forward(hs, q_w, q_b, k_w, k_b, v_w, v_b, o_w, o_b, router_w, router_b, w1, b1, w2, b2):
            B, S, _ = hs.shape
            Q = (hs @ q_w + q_b).reshape(B, S, H, HD).transpose(0, 2, 1, 3)
            K = (hs @ k_w + k_b).reshape(B, S, H, KPH).transpose(0, 2, 1, 3)
            V = (hs @ v_w + v_b).reshape(B, S, H, KPH).transpose(0, 2, 1, 3)
            scores = jnp.einsum('bhsk,bhtk->bhst', Q[..., :KPH], K) / math.sqrt(KPH)
            attn = jax.nn.softmax(scores, axis=-1)
            ao = jnp.einsum('bhst,bhtv->bhsv', attn, V)
            ao = ao.transpose(0, 2, 1, 3).reshape(B, S, H * KPH)
            ao = jnp.concatenate([ao, jnp.zeros((B, S, D - LAT), ao.dtype)], axis=-1)
            mla_out = ao @ o_w + o_b
            probs = jax.nn.softmax(mla_out @ router_w + router_b, axis=-1)
            topw, topi = jax.lax.top_k(probs, TOPK)
            topw = topw / (topw.sum(-1, keepdims=True) + 1e-08)
            combine = jnp.sum(jax.nn.one_hot(topi, E, dtype=probs.dtype) * topw[..., None], axis=-2)
            h1 = jnp.einsum('bsd,edf->ebsf', mla_out, w1) + b1[:, None, None, :]
            h1 = jax.nn.gelu(h1, approximate=False)
            h2 = jnp.einsum('ebsf,efd->ebsd', h1, w2) + b2[:, None, None, :]
            moe_out = jnp.einsum('bse,ebsd->bsd', combine, h2)
            return hs + 0.3 * moe_out
        return _forward(hidden_states, q_w, q_b, k_w, k_b, v_w, v_b, o_w, o_b, router_w, router_b, w1, b1, w2, b2)

    def _L1_attn_ref(x, wq, wk, wv, wo, q_norm_w, k_norm_w):
        import jax, jax.numpy as jnp
        import numpy as np
        import math
        B, T, DIM = (4, 256, 128)
        N_HEADS, HEAD_DIM = (8, 128)
        WINDOW = 16
        EPS = 1e-06
        NEG = -1000000000.0

        def _alibi_slopes(n_heads):
            r = 2.0 ** (-8.0 / n_heads)
            return jnp.asarray([r ** i for i in range(n_heads)], dtype=jnp.float32)

        def _rms_norm(x, w, eps):
            var = jnp.mean(jnp.square(x), axis=-1, keepdims=True)
            return x * jax.lax.rsqrt(var + eps) * w
        Bx, Tx, _ = x.shape
        xq = _rms_norm(x @ wq, q_norm_w, EPS)
        xk = _rms_norm(x @ wk, k_norm_w, EPS)
        xv = x @ wv
        q = xq.reshape(Bx, Tx, N_HEADS, HEAD_DIM).transpose(0, 2, 1, 3)
        k = xk.reshape(Bx, Tx, N_HEADS, HEAD_DIM).transpose(0, 2, 1, 3)
        v = xv.reshape(Bx, Tx, N_HEADS, HEAD_DIM).transpose(0, 2, 1, 3)
        pos = jnp.arange(Tx)
        rel = pos[None, :] - pos[:, None]
        slopes = _alibi_slopes(N_HEADS)
        bias = slopes[:, None, None] * rel.astype(jnp.float32)
        invalid = (rel > 0) | (rel < -WINDOW)
        bias = jnp.where(invalid[None, :, :], NEG, bias)
        scale = 1.0 / math.sqrt(HEAD_DIM)
        scores = jnp.einsum('bhqd,bhkd->bhqk', q, k) * scale + bias[None]
        probs = jax.nn.softmax(scores, axis=-1)
        y = jnp.einsum('bhqk,bhkd->bhqd', probs, v)
        y = y.transpose(0, 2, 1, 3).reshape(Bx, Tx, N_HEADS * HEAD_DIM)
        return y @ wo

    def _L1_xattn_ref(query, context, mask, Wq, bq, Wkv, bkv, Wout, bout, num_heads):
        import jax, jax.numpy as jnp
        import numpy as np
        B, SQ, SKV, D, H = (2, 256, 256, 128, 16)
        HD = D // H

        def cross_attention(query, context, mask, Wq, bq, Wkv, bkv, Wout, bout, num_heads):
            b, sq, d = query.shape
            skv = context.shape[1]
            hd = d // num_heads
            scale = hd ** (-0.5)
            q = query @ Wq + bq
            kv = context @ Wkv + bkv
            kv = kv.reshape(b, skv, 2, num_heads, hd).transpose(2, 0, 3, 1, 4)
            k, v = (kv[0], kv[1])
            q = q.reshape(b, sq, num_heads, hd).transpose(0, 2, 1, 3)
            scores = jnp.einsum('bhid,bhjd->bhij', q, k) * scale
            scores = jnp.where(mask[:, None, None, :], -jnp.inf, scores)
            attn = jax.nn.softmax(scores, axis=-1)
            out = jnp.einsum('bhij,bhjd->bhid', attn, v)
            out = out.transpose(0, 2, 1, 3).reshape(b, sq, d)
            return out @ Wout + bout
        return cross_attention(query, context, mask, Wq, bq, Wkv, bkv, Wout, bout, num_heads)

    def _L1_ffn_ref(x, w_gate, w_up, w_down):
        import jax, jax.numpy as jnp
        import numpy as np
        BLOCK = 16
        _GRID = jnp.array([0.0, 0.5, 1.0, 1.5, 2.0, 3.0, 4.0, 6.0], dtype=jnp.float32)
        _MID = jnp.array([0.25, 0.75, 1.25, 1.75, 2.5, 3.5, 5.0], dtype=jnp.float32)

        def fp4_quant_dequant(x):
            shape = x.shape
            xb = x.reshape(shape[:-1] + (shape[-1] // BLOCK, BLOCK))
            scale = jnp.max(jnp.abs(xb), axis=-1, keepdims=True) / 6.0
            scale = jnp.maximum(scale, jnp.float32(1e-12))
            xn = xb / scale
            idx = jnp.searchsorted(_MID, jnp.abs(xn))
            q = _GRID[idx] * jnp.sign(xn) * scale
            return q.reshape(shape)

        def fp4_linear(x, w):
            xq = fp4_quant_dequant(x)
            wq = fp4_quant_dequant(w)
            return jnp.einsum('bsk,nk->bsn', xq, wq)
        gate = fp4_linear(x, w_gate)
        y = fp4_linear(x, w_up)
        h = jax.nn.silu(gate) * y
        return fp4_linear(h, w_down)
    x = x + _L0_attn_ref(_layernorm(x, axis=-1), L0_attn_W_in, L0_attn_b_in, L0_attn_W_out, L0_attn_b_out)
    x = x + _L0_xattn_ref(_layernorm(x, axis=-1), ctx_1024, ctx_1024, mask_1xSxS2_ff0, L0_xattn_kernel_q, L0_xattn_kernel_k, L0_xattn_kernel_v, L0_xattn_bias_q, L0_xattn_bias_k, L0_xattn_bias_v)
    x = x + _L0_ffn_ref(_layernorm(x, axis=-1), L0_ffn_q_w, L0_ffn_q_b, L0_ffn_k_w, L0_ffn_k_b, L0_ffn_v_w, L0_ffn_v_b, L0_ffn_o_w, L0_ffn_o_b, L0_ffn_router_w, L0_ffn_router_b, L0_ffn_w1, L0_ffn_b1, L0_ffn_w2, L0_ffn_b2)
    x = x + _L1_attn_ref(_layernorm(x, axis=-1), L1_attn_wq, L1_attn_wk, L1_attn_wv, L1_attn_wo, L1_attn_q_norm_w, L1_attn_k_norm_w)
    x = x + _L1_xattn_ref(_layernorm(x, axis=-1), ctx_1024, mask_BxS2_bf0, L1_xattn_Wq, L1_xattn_bq, L1_xattn_Wkv, L1_xattn_bkv, L1_xattn_Wout, L1_xattn_bout, 16)
    x = x + _L1_ffn_ref(_layernorm(x, axis=-1), L1_ffn_w_gate, L1_ffn_w_up, L1_ffn_w_down)
    return x

_drawn_inputs = setup_inputs


def setup_inputs(seed=0):
    import zlib

    import numpy as np

    out = dict(_drawn_inputs(seed))
    spreads = {'L0_attn_b_in': (0.0, 0.411),
     'L0_attn_b_out': (0.0, 0.424),
     'L0_ffn_q_b': (0.0, 2.0),
     'L0_ffn_k_b': (0.0, 2.0),
     'L0_ffn_v_b': (0.0, 0.8),
     'L0_ffn_o_b': (0.0, 0.8),
     'L0_ffn_router_b': (0.0, 2.0),
     'L0_ffn_b1': (0.0, 0.8),
     'L0_ffn_b2': (0.0, 2.0),
     'L1_attn_q_norm_w': (1.0, 0.6),
     'L1_attn_k_norm_w': (1.0, 0.6),
     'L1_xattn_bq': (0.0, 0.8),
     'L1_xattn_bkv': (0.0, 0.8),
     'L1_xattn_bout': (0.0, 0.8)}
    factors = {'L0_attn_W_in': 2.675,
     'L0_attn_W_out': 2.805,
     'L0_xattn_bias_q': 5.905,
     'L0_xattn_bias_k': 6.132,
     'L0_ffn_q_w': 27.917,
     'L0_ffn_k_w': 27.67,
     'L0_ffn_v_w': 8.0,
     'L0_ffn_o_w': 8.0,
     'L0_ffn_router_w': 8.0,
     'L0_ffn_w1': 8.0,
     'L0_ffn_w2': 8.0,
     'L1_attn_wq': 24.091,
     'L1_attn_wk': 24.157,
     'L1_xattn_Wq': 5.917,
     'L1_xattn_Wkv': 2.783,
     'L1_ffn_w_gate': 8.0,
     'L1_ffn_w_up': 8.0,
     'L1_ffn_w_down': 8.0}
    for name, (base, spread) in spreads.items():
        noise = np.random.default_rng([zlib.crc32(name.encode()), seed]).standard_normal(out[name].shape)
        drawn = base * np.exp(spread * noise) if base else spread * noise
        out[name] = jnp.asarray(drawn.astype(out[name].dtype))
    for name, factor in factors.items():
        out[name] = (out[name] * factor).astype(out[name].dtype)
    return out
```

```python
from contextlib import ExitStack

import numpy as np
import concourse.bass as bass
from concourse import mybir

P = 128
B = 4
S = 512
QT = S // P
CK = 32
BANK = 512
BANKS = 8
H0, E0 = 16, 64
PAIRS = H0 // 2
UNITS = B * PAIRS
EPS0 = 1e-4
HC, KPH, HDC = 16, 4, 8
GROUPS = HC // 4
NE, FE = 8, 256
HD1 = 8
WINDOW = 16
NEG = -1e9
TILES1 = [(0, 128, 0, 0), (128, 112, 112, 1), (240, 112, 224, 1), (352, 112, 336, 1), (464, 48, 384, 2)]
HX, DX = 16, 8
FI = 352
FCH = [(0, 128), (128, 128), (256, 96)]
BLK = 16

ALU = mybir.AluOpType
ACT = mybir.ActivationFunctionType
AX = mybir.AxisListType
F32 = mybir.dt.float32
BF16 = mybir.dt.bfloat16
U32 = mybir.dt.uint32
U8 = mybir.dt.uint8


def constant_columns():
    cols = {}
    part = np.arange(P)
    cols["ident"] = np.eye(P)
    half = part // E0
    cols["pairsum"] = (half[:, None] == half[None, :]).astype(np.float32)
    cols["ones"] = np.ones((P, P))
    row, head = part % 32, part // 32
    term = row // KPH
    q_part = np.array([0, 0, 1, 0, 2, 1, 0, 0])[term]
    k_part = np.array([0, 1, 0, 2, 0, 1, 0, 0])[term]
    for name, which in (("q", q_part), ("k", k_part)):
        cols[f"{name}_less_high"] = -(which >= 1).astype(np.float32)[:, None]
        cols[f"{name}_less_mid"] = -(which == 2).astype(np.float32)[:, None]
    cols["head_rows"] = (head[:, None] == np.arange(4)[None, :]).astype(np.float32)
    cols["eps_w"] = np.full((P, 1), EPS0)
    cols["eps_ln"] = np.full((P, 1), 1e-5)
    cols["eps_rms"] = np.full((P, 1), 1e-6)
    cols["xhead"] = (part[:, None] // DX == np.arange(HX)[None, :]).astype(np.float32)
    vmask = np.zeros((P, 4, P))
    for g in range(4):
        vmask[:, g, :] = (part[None, :] // DX == (4 * g + head)[:, None])
    cols["vhead"] = vmask.reshape(P, -1)
    cols["turn"] = np.tile(np.arange(NE, 0, -1)[None, :], (P, 1))
    return cols


def window_bias():
    slopes = (2.0 ** (-8.0 / HD1)) ** np.arange(HD1)
    out = np.zeros((3, P, HD1, P), np.float32)
    for kind, off in enumerate((0, 16, 80)):
        rel = np.arange(P)[None, :] - off - np.arange(P)[:, None]
        for h in range(HD1):
            out[kind, :, h, :] = np.where((rel > 0) | (rel < -WINDOW), NEG, slopes[h] * rel)
    return out.transpose(1, 0, 2, 3).reshape(P, -1)


def constant_places():
    at, places = 0, {}
    for name, a in constant_columns().items():
        places[name] = (at, a.shape[1])
        at += a.shape[1]
    return places, at


def psum_jobs():
    jobs = [(("tb", i), 1, [("bias_cols", i + 1)]) for i in range(2)]
    jobs += [(("ln", 0, b), 1, [("xt_ready", b + 1)]) for b in range(B)]

    def project(u):
        return [(("QA", u), 1, [("mq_scaled", 2 * u + 1), ("mq_squared", 2 * u + 1)]),
                (("QB", u), 1, [("mq_scaled", 2 * u + 2), ("mq_squared", 2 * u + 2)]),
                (("K", u), 1, [("k_sb", 2 * u + 2)]), (("V", u), 1, [("v_sb", u + 1)]),
                (("G", u), 1, [("g_sb", u + 1)])]

    def key_norms(u):
        return [(("k2", u), 1, [("k2_sb", u + 1)])]

    def weighted_values(u):
        return [(("PV", u), 1, [("h_done", u + 1)]), (("RS", u), 1, [("rs_log", u + 1)])]

    jobs += project(0) + key_norms(0)
    for u in range(UNITS):
        jobs += [(("S", u, c), 1, [("guarded", 8 * u + c + 1)]) for c in range(8)]
        if u + 1 < UNITS:
            jobs += project(u + 1)
        if u >= 1:
            jobs += weighted_values(u - 1)
        if u + 1 < UNITS:
            jobs += key_norms(u + 1)
        if u >= 2 and (u - 2) % PAIRS == PAIRS - 1:
            jobs += [(("out0", (u - 2) // PAIRS), 1, [("x_new", (u - 2) // PAIRS + 1)])]
    jobs += weighted_values(UNITS - 1) + [(("out0", B - 1), 1, [("x_new", B)])]
    jobs += [(("xmask", 0), 1, [("mask_sb", 1)]), (("ctxT", 0), 1, [("ctxT_sb", 1)]),
             (("xk", 0), 1, [("xk_sb", 1)]), (("xv", 0), 1, [("xv_sum", 1)])]
    jobs += [(("ln", 1, b), 1, [("xt_ready", B + b + 1)]) for b in range(B)]
    jobs += [(("xq", b), 1, [("xq_sb", b + 1)]) for b in range(B)]
    jobs += [(("xs", b), 1, [("xs_relu", b + 1)]) for b in range(B)]
    jobs += [(("xo", b), 1, [("x_new", B + b + 1)]) for b in range(B)]
    jobs += [(("ln", 2, b), 1, [("xt_ready", 2 * B + b + 1)]) for b in range(B)]
    jobs += stage_c_jobs()
    jobs += stage_d_jobs()
    jobs += stage_e_jobs()
    jobs += stage_f_jobs()
    return jobs


def stage_c_jobs():
    jobs = [(("tb", 2), 1, [("expand_cols", 1)])]

    def prepare(w):
        value = [(("cV", w // GROUPS), 1, [("c_v", w // GROUPS + 1)])] if w % GROUPS == 0 else []
        return value + [(("cQ", w), 1, [("c_high", 2 * w + 1)]), (("cK", w), 1, [("c_high", 2 * w + 2)])]

    def maxima(w, i):
        return [(("cS", w, i), 2, [("c_max", 8 * w + i + 1)])]

    def turned_max(w):
        return [(("cM", w), 1, [("c_qm", w + 1)])]

    def back(w):
        b, g = divmod(w, GROUPS)
        return [(("cA", w), 1, [("c_ao", w + 1)])] + (
            [(("cT", b), 1, [("c_aot", b + 1)]), (("cO", b), 1, [("c_mla", b + 1)])] if g == GROUPS - 1 else [])

    last = B * GROUPS - 1
    jobs += prepare(0)
    for i in range(8):
        jobs += maxima(0, i)
    jobs += prepare(1) + turned_max(0)
    for w in range(last + 1):
        for i in range(8):
            if w < last:
                jobs += maxima(w + 1, i)
            jobs += [(("cP", w, i), 2, [("c_exp", 8 * w + i + 1)])]
        if w + 2 <= last:
            jobs += prepare(w + 2)
        if w < last:
            jobs += turned_max(w + 1)
        jobs += [(("cV4", w), 1, [("c_aos", w + 1)])]
        if w:
            jobs += back(w - 1)
    jobs += back(last)
    jobs += [(("rt", 0), 1, [("r_logits", 1)])]
    jobs += [(("rc", b), 1, [("r_ct", b + 1)]) for b in range(B)]
    jobs += [(("h1", 0, c), 1, [("h1_ready", c + 1)]) for c in range(2)]
    for i in range(B * NE):
        if i + 1 < B * NE:
            jobs += [(("h1", i + 1, c), 1, [("h1_ready", 2 * (i + 1) + c + 1)]) for c in range(2)]
        if i % NE == 0:
            jobs += [(("b2", i // NE), 1, [("acc_set", i // NE + 1)])]
        jobs += [(("h2", i), 1, [("weighed", i + 1)])]
    return jobs


def stage_d_jobs():
    jobs = [(("gt", i), 1, [("gram_turned", i + 1)]) for i in range(4)]
    jobs += [(("gg", m), 1, [("gram", m + 1)]) for m in range(2)]
    jobs += [(("ln", 3, b), 1, [("xt_ready", 3 * B + b + 1)]) for b in range(B)]
    jobs += [(("z", b, m), 1, [("zy", 2 * b + m + 1)]) for b in range(B) for m in range(2)]
    jobs += [(("yt", 0, m), 1, [("xqk", m + 1)]) for m in range(2)]
    steps = B * len(TILES1)

    def start(n):
        b, ti = divmod(n, len(TILES1))
        out = []
        if ti == 0:
            for h in range(HD1):
                out += [(("dQ", b, h), 1, [("d_q", HD1 * b + h + 1)]), (("dK", b, h), 1, [("d_k", HD1 * b + h + 1)])]
            if b + 1 < B:
                out += [(("yt", b + 1, m), 1, [("xqk", 2 * (b + 1) + m + 1)]) for m in range(2)]
        return out + [(("dS", n), 2, [("d_biased", n + 1)]), (("dV", n), 2, [("d_v", n + 1)])]

    def finish(n):
        out = [(("dY", n), 2, [("d_y", n + 1)])]
        b, ti = divmod(n, len(TILES1))
        return out + ([(("out1", b), 1, [("x_new", 3 * B + b + 1)])] if ti == len(TILES1) - 1 else [])

    jobs += start(0) + start(1)
    for n in range(steps):
        if n + 2 < steps:
            jobs += start(n + 2)
        if n:
            jobs += finish(n - 1)
        jobs += [(("dT", n), 2, [("d_pt", n + 1)])]
    return jobs + finish(steps - 1)


def stage_e_jobs():
    jobs = [(("eK", 0), 1, [("e_k", 1)])]
    jobs += [(("eV", b), 1, [("e_v4", b + 1)]) for b in range(B)]
    jobs += [(("ln", 4, b), 1, [("xt_ready", 4 * B + b + 1)]) for b in range(B)]
    jobs += [(("eQ", b), 1, [("e_q", b + 1)]) for b in range(B)]
    steps = B * QT
    jobs += [(("eS", n), 1, [("e_biased", n + 1)]) for n in range(2)]
    for n in range(steps):
        if n + 2 < steps:
            jobs += [(("eS", n + 2), 1, [("e_biased", n + 3)])]
        jobs += [(("eT", n), 1, [("e_pt", n + 1)])]
        if n % QT == QT - 1:
            b = n // QT
            jobs += [(("eO", b), 1, [("e_o", b + 1)]), (("eX", b), 1, [("x_new", 4 * B + b + 1)])]
    return jobs


def stage_f_jobs():
    jobs = [(("fW", i), 1, [("f_w", i + 1)]) for i in range(3)]
    jobs += [(("fX", b), 1, [("f_x", b + 1)]) for b in range(B)]
    steps = B * QT

    def start(n):
        return [(("fG", n), 1, [("f_silu", n + 1)]), (("fU", n), 1, [("f_h", n + 1)])]

    jobs += start(0) + start(1)
    for n in range(steps):
        if n + 2 < steps:
            jobs += start(n + 2)
        if n:
            jobs += [(("fD", n - 1), 1, [("x_final", n)])]
        jobs += [(("fT", n), 1, [("f_ht", n + 1)])]
    return jobs + [(("fD", steps - 1), 1, [("x_final", steps)])]


def place_jobs(jobs):
    pos = 0
    fulls, user, placed = [0] * BANKS, [[]] * BANKS, {}
    for key, size, read in jobs:
        pos += -pos % size
        k = pos % BANKS
        waits = {}
        for j in range(k, k + size):
            for name, value in user[j]:
                waits[name] = max(waits.get(name, 0), value)
            user[j] = read
        fulls[k] += 1
        placed[key] = (k, size, fulls[k], waits)
        pos += size
    return placed


def decoder_kernel(nc, a, out, stop=6):
    places, n_consts = constant_places()
    placed = place_jobs(psum_jobs())

    with ExitStack() as ctx:
        def sb(name, shape, dt=F32):
            return ctx.enter_context(nc.sbuf_tensor(name, shape, dt))

        sems = {}

        def sem(name):
            if name not in sems:
                sems[name] = ctx.enter_context(nc.semaphore(name))
            return sems[name]

        PS = ctx.enter_context(nc.psum_tensor("PS", [P, BANKS, BANK], F32))
        full_sem = [ctx.enter_context(nc.semaphore(f"bank_full{k}")) for k in range(BANKS)]

        def bank(key):
            k, size = placed[key][:2]
            return PS[:, k, :] if size == 1 else PS[:, k:k + size, :]

        def full(eng, key):
            k, _, value, _ = placed[key]
            eng.wait_ge(full_sem[k], value)

        C = sb("consts_sb", [P, n_consts])

        def const(name):
            at, n = places[name]
            return C[:, at:at + n]

        ident = const("ident")
        identb = sb("identb", [P, P], BF16)
        X = sb("X", [P, B, QT, P])
        Y = sb("Y", [P, B, QT, P])
        XT = sb("XT", [P, B, S])
        STAT = sb("STAT", [P, B, QT, 6])
        MV = sb("MV", [P, B, QT, 2])
        RSTD = sb("RSTD", [P, B, 2, QT])
        BROW = sb("BROW", [64, P])
        NROW = sb("NROW", [64, P])
        BT0 = sb("BT0", [P, 64])
        BN = sb("BN", [P, 64])
        NCOL = {}
        n = 0
        for name, rows in (("L0_xattn_bias_q", 1), ("L0_xattn_bias_k", 1), ("L0_ffn_o_b", 1),
                           ("L0_ffn_b1", 16), ("L1_attn_q_norm_w", 8), ("L1_attn_k_norm_w", 8),
                           ("L1_xattn_bq", 1), ("L1_xattn_bkv", 2)):
            NCOL[name] = n
            n += rows
        WQ = sb("WQ", [P, H0, 2, E0])
        WKVG = sb("WKVG", [P, 3, H0, E0])
        Wout = sb("Wout", [P, PAIRS, P])
        BV = sb("BV", [P, H0, E0])
        Bout = sb("Bout", [P, P])
        XK = sb("XK", [P, 3, P])
        BXV = sb("BXV", [P, P])
        CTX = sb("CTX", [P, P])
        CTXT = sb("CTXT", [P, P])
        QW = sb("QW", [P, P])
        KW = sb("KW", [P, HC * KPH])
        VW = sb("VW", [P, HC * KPH])
        BVC = sb("BVC", [P, HC * KPH])
        OW = sb("OW", [P, P])
        RW = sb("RW", [P, NE])
        RB = sb("RB", [P, NE])
        W1 = sb("W1", [P, NE, FE])
        W2 = sb("W2", [P, NE, 2, P])
        B2 = sb("B2", [NE, P])
        QKROW = sb("QKROW", [1, 2 * GROUPS, P])
        BQK = sb("BQK", [P, 2 * GROUPS])
        ARENA = sb("ARENA", [P, 27900])

        def carve(at, shape, dt=F32):
            n = int(np.prod(shape))
            words = n if dt == F32 else n // 2
            t = ARENA[:, at:at + words]
            if dt != F32:
                t = t.bitcast(dt)
            if len(shape) > 1:
                names = "abcd"[:len(shape)]
                t = t.rearrange(f"p ({' '.join(names)}) -> p {' '.join(names)}",
                                **{c: s for c, s in zip(names, shape)})
            return t, at + words

        HT, at = carve(0, [2, PAIRS, S])
        D, at = carve(at, [2, 2, QT, S])
        MQ, at = carve(at, [2, S])
        SK, at = carve(at, [2, S])
        KSQ, at = carve(at, [S])
        VA, at = carve(at, [3, QT, P])
        GA, at = carve(at, [3, S])
        LR, at = carve(at, [S])
        RR, at = carve(at, [S])
        GR, at = carve(at, [S])
        K2, at = carve(at, [2, QT, 2])
        MSK = sb("MSK", [P, QT, P])
        MT, at2 = carve(0, [S])
        xqT, at2 = carve(at2, [B, S])
        xkT, at2 = carve(at2, [P])
        xv, at2 = carve(at2, [P])
        xtmp, at2 = carve(at2, [P])
        LT, at2 = carve(at2, [B, S])

        WX, at = carve(0, [2, GROUPS, P])
        VC, at = carve(at, [2, QT, HC, 32])
        V32, at = carve(at, [2, S])
        HI, at = carve(at, [2, S], BF16)
        R1, at = carve(at, [2, S])
        MID, at = carve(at, [2, S], BF16)
        KST, at = carve(at, [S], BF16)
        QS, at = carve(at, [2, S], BF16)
        KM, at = carve(at, [2, 4, S], BF16)
        NMX, at = carve(at, [2, QT, 4])
        RMX, at = carve(at, [QT, 4])
        TMX, at = carve(at, [2, QT, P], BF16)
        AOS, at = carve(at, [2, S])
        RCP, at = carve(at, [QT, 4])
        AOTOK, at = carve(at, [2, QT, HC * KPH])
        AOT, at = carve(at, [S])
        PT_SLOTS = 12
        PT, end = carve(at, [PT_SLOTS, 2, S])
        CT, at = carve(at, [B, S])
        ACC, at = carve(at, [2, S])
        TMP, at = carve(at, [2, S])
        H1, at = carve(at, [2, 2, S])
        RT = []
        for _ in range(12):
            t, at = carve(at, [B * QT, NE])
            RT.append(t)
        RS1 = []
        for _ in range(8):
            t, at = carve(at, [B * QT])
            RS1.append(t)

        flat_q = WQ[:].rearrange("p h a e -> p (h a e)")
        flat_kvg = WKVG[:].rearrange("p k h e -> p (k h e)")
        WQK1 = [flat_q[:, 0:1024], flat_q[:, 1024:2048]]
        WV1 = flat_kvg[:, 0:1024]
        WO1 = flat_kvg[:, 1024:2048].rearrange("p (h d) -> p h d", h=HD1)
        GM = flat_kvg[:, 2048:2304].rearrange("p (m d) -> p m d", m=2)
        QT1, at = carve(0, [HD1, S])
        KT1, at = carve(at, [HD1, S])
        V1, at = carve(at, [4, HD1 * P])
        SM, at = carve(at, [3, HD1, P])
        PT1, at = carve(at, [2, HD1, P])
        YT1, at = carve(at, [HD1, S])
        XQK, at = carve(at, [2, 2, S])
        YM, at = carve(at, [2, QT, P])
        NM1, at = carve(at, [3, HD1])
        SUM1, at = carve(at, [3, HD1])
        RC1, at = carve(at, [3, HD1])
        SS, at = carve(at, [B, 2, QT])
        RL, at = carve(at, [B, 2, QT])
        RMS, at = carve(at, [B, 2, QT])
        BM, at = carve(at, [3, HD1, P])
        WT = [SM.rearrange("p a h q -> p (a h q)")[:, i * 1024:(i + 1) * 1024].rearrange("p (c d) -> p c d", c=8) for i in range(2)]
        ZY = YM
        flat_w1 = W1[:].rearrange("p e f -> p (e f)")
        flat_w2 = W2[:].rearrange("p e c d -> p (e c d)")
        EW, FW = {}, {}
        at = 0
        for name, n in (("q", P), ("k", P), ("v", P), ("out", P), ("bias_v", P), ("bias_out", P)):
            EW[name] = flat_w1[:, at:at + n]
            at += n
        at = 0
        for name, n in (("gate", 3 * P), ("up", 3 * P), ("down", FI)):
            FW[name] = flat_w2[:, at:at + n]
            at += n
        MK8 = sb("MK8", [P, B * CK], U8)
        MB = sb("MB", [P, B, CK])
        SIGN = sb("SIGN", [P, 1], U32)
        KTX, at = carve(0, [B, CK])
        CT4, at = carve(at, [B, 4 * CK])
        V4, at = carve(at, [2, P])
        VX, at = carve(at, [B, 4, P])
        KX, at = carve(at, [B, HX, CK])
        QTX, at = carve(at, [B, S])
        SE, at = carve(at, [3, HX, CK])
        PE1, at = carve(at, [3, HX, CK])
        NME, at = carve(at, [2, HX])
        SUE, at = carve(at, [2, HX])
        RCE, at = carve(at, [2, HX])
        PTE, at = carve(at, [2, 4, S])
        OTE, at = carve(at, [2, S])
        WGU, at = carve(at, [2, FI])
        WD, at = carve(at, [3, P])
        QSC, at = carve(at, [4, 32])
        QA_, at = carve(at, [512])
        QB_, at = carve(at, [512])
        QC_, at = carve(at, [512])
        QD_, at = carve(at, [512])
        WQT, at = carve(at, [3, 3 * P])
        YQ, at = carve(at, [2, QT, P])
        XQT, at = carve(at, [B, S])
        SG, at = carve(at, [3, FI])
        HF, at = carve(at, [FI])
        HQ, at = carve(at, [2, FI])
        HQT, at = carve(at, [2, 3, P])

        for name in ("d_weights_in", "bias_in", "e_weights_in", "gram_turned", "gram", "zy", "ss", "r_log", "r_rms", "ym",
                     "xqk", "d_q", "d_k", "d_biased", "d_v", "d_max", "d_exp", "d_norm", "d_pt", "d_y", "e_k", "e_v4",
                     "e_vx", "e_kx", "e_ctx4", "e_q", "e_biased", "e_shift", "e_exp", "e_rc", "e_p", "e_pt", "e_o", "xb4",
                     "mask_bias", "f_wq", "f_w", "f_yq", "f_x", "f_silu", "f_h", "f_hq", "f_ht", "x_final"):
            sem(name)
        for name in ("expand_rows_in", "expand_cols", "expanded", "c_init", "c_v", "c_v32", "c_high", "c_qs", "c_km", "c_max",
                     "c_tmx", "c_qm", "c_exp", "c_aos", "c_ao", "c_aot", "c_mla", "r_logits", "r_shift", "r_exp",
                     "r_comb", "r_ct", "h1_ready", "acc_set", "weighed", "summed", "cw_in", "row_set", "xy"):
            sem(name)
        for name in ("loaded", "out_done", "consts_in", "x_in", "win_in", "rows_in", "bcast_in", "xw_in", "identb_ready",
                     "bias_cols", "ln_stats", "ln_log", "ln_rstd", "ln_y", "xt_ready", "dve_chain",
                     "mq_scaled", "mq_squared", "k_sb", "ksq", "v_sb", "g_sb", "k2_sb", "guarded", "rooted",
                     "logged", "w_ready", "rs_log", "rs_inv", "gr", "h_done", "x_biased", "x_new",
                     "mask_sb", "ctxT_sb", "xk_sb", "xv_sum", "xv_sb", "xq_sb", "xs_relu", "logits"):
            sem(name)

        block = ctx.enter_context(nc.Block())

        def tensor_c(pe, begin, done):
            last = B * GROUPS - 1
            pe.wait_ge(sem("expand_rows_in"), 16 * 48)
            o = begin(("tb", 2))
            for i in range(2 * GROUPS):
                mm = pe.transpose(o[:, i:i + 1], QKROW[:, i, :], ident[0:1, 0:1])
            done(mm, ("tb", 2))

            def prepare(w):
                b, g = divmod(w, GROUPS)
                if g == 0:
                    pe.wait_ge(sem("xt_ready"), 2 * B + b + 1)
                    o = begin(("cV", b))
                    for kt in range(QT):
                        mm = pe.matmul(o[:, kt * 64:kt * 64 + 64], XT[:, b, kt * P:(kt + 1) * P], VW[:],
                                       start=True, stop=True)
                    done(mm, ("cV", b))
                for side, key in enumerate(("cQ", "cK")):
                    o = begin((key, w))
                    done(pe.matmul(o, WX[:, side, g, :], XT[:, b], start=True, stop=True), (key, w))

            def maxima(w, i):
                t, jp = divmod(i, 2)
                if i == 0:
                    pe.wait_ge(sem("c_qs"), w + 1)
                    pe.wait_ge(sem("c_km"), w + 1)
                o = begin(("cS", w, i))
                for j in range(2):
                    mm = pe.matmul(o[:, j, :], QS[:, w % 2, t * P:(t + 1) * P], KM[:, w % 2, 2 * jp + j, :],
                                   start=True, stop=True)
                done(mm, ("cS", w, i))

            def turned_max(w):
                pe.wait_ge(sem("c_tmx"), w + 1)
                o = begin(("cM", w)).bitcast(BF16)
                for t in range(QT):
                    mm = pe.transpose(o[:, t * P:(t + 1) * P], TMX[:, w % 2, t, :], identb[:])
                done(mm, ("cM", w))

            def shifted(w, i):
                kp, j = divmod(i, 4)
                if i == 0:
                    pe.wait_ge(sem("c_qm"), w + 1)
                o = begin(("cP", w, i))
                for k in range(2):
                    kt = 2 * kp + k
                    mm = pe.matmul(o[:, k, :], KM[:, w % 2, j, kt * P:(kt + 1) * P], QS[:, w % 2, :],
                                   start=True, stop=True)
                done(mm, ("cP", w, i))

            def values(w):
                b, g = divmod(w, GROUPS)
                pe.wait_ge(sem("c_v"), b + 1)
                o = begin(("cV4", w))
                for kt in range(QT):
                    for j in range(4):
                        n = 8 * w + 4 * (kt // 2) + j
                        pe.wait_ge(sem("c_exp"), n + 1)
                        mm = pe.matmul(o[32 * j:32 * j + 32, :], VC[:, b % 2, kt, 4 * g + j, :],
                                       PT[:, n % PT_SLOTS, kt % 2, :], start=kt == 0, stop=kt == QT - 1)
                done(mm, ("cV4", w))

            def back(w):
                b, g = divmod(w, GROUPS)
                pe.wait_ge(sem("c_aos"), w + 1)
                o = begin(("cA", w))
                for t in range(QT):
                    mm = pe.transpose(o[:, t * P:(t + 1) * P], AOS[:, w % 2, t * P:(t + 1) * P], ident)
                done(mm, ("cA", w))
                if g == GROUPS - 1:
                    pe.wait_ge(sem("c_ao"), w + 1)
                    o = begin(("cT", b))
                    for t in range(QT):
                        mm = pe.transpose(o[0:64, t * P:(t + 1) * P], AOTOK[:, b % 2, t, :], ident)
                    done(mm, ("cT", b))
                    pe.wait_ge(sem("c_aot"), b + 1)
                    o = begin(("cO", b))
                    done(pe.matmul(o, OW[:], AOT, start=True, stop=True), ("cO", b))

            pe.wait_ge(sem("cw_in"), 160)
            pe.wait_ge(sem("expanded"), 2)
            pe.wait_ge(sem("c_init"), 3)
            prepare(0)
            for i in range(8):
                maxima(0, i)
            prepare(1)
            turned_max(0)
            for w in range(last + 1):
                for i in range(8):
                    if w < last:
                        maxima(w + 1, i)
                    shifted(w, i)
                if w + 2 <= last:
                    prepare(w + 2)
                if w < last:
                    turned_max(w + 1)
                values(w)
                if w:
                    back(w - 1)
            back(last)

            o = begin(("rt", 0))
            for b in range(B):
                pe.wait_ge(sem("c_mla"), b + 1)
                for t in range(QT):
                    n = b * QT + t
                    mm = pe.matmul(o[:, n * NE:(n + 1) * NE], XT[:, b, t * P:(t + 1) * P], RW[:], start=True, stop=True)
            done(mm, ("rt", 0))
            pe.wait_ge(sem("r_comb"), 1)
            for b in range(B):
                o = begin(("rc", b))
                for t in range(QT):
                    mm = pe.transpose(o[0:NE, t * P:(t + 1) * P], RT[11][:, b * QT + t, :], ident)
                done(mm, ("rc", b))

            def up(i):
                b, e = divmod(i, NE)
                for c in range(2):
                    o = begin(("h1", i, c))
                    done(pe.matmul(o, W1[:, e, c * P:(c + 1) * P], XT[:, b], start=True, stop=True), ("h1", i, c))

            up(0)
            for i in range(B * NE):
                b, e = divmod(i, NE)
                if i + 1 < B * NE:
                    up(i + 1)
                if e == 0:
                    pe.wait_ge(sem("r_ct"), b + 1)
                    o = begin(("b2", b))
                    for t in range(QT):
                        mm = pe.matmul(o[:, t * P:(t + 1) * P], CT[0:NE, b, t * P:(t + 1) * P], B2[:], start=True, stop=True)
                    done(mm, ("b2", b))
                pe.wait_ge(sem("h1_ready"), 2 * i + 2)
                o = begin(("h2", i))
                for t in range(QT):
                    for c in range(2):
                        mm = pe.matmul(o[:, t * P:(t + 1) * P], H1[:, i % 2, c, t * P:(t + 1) * P], W2[:, e, c, :],
                                       start=c == 0, stop=c == 1)
                done(mm, ("h2", i))

        def scalar_c(act):
            last = B * GROUPS - 1

            def prepare(w):
                g = w % GROUPS
                for side, key in enumerate(("cQ", "cK")):
                    full(act, (key, w))
                    if w:
                        act.wait_ge(sem("c_qs" if side == 0 else "c_km"), w)
                    c = side * GROUPS + g
                    act.activation(V32[:, side], bank((key, w)), ACT.Identity,
                                   bias=BQK[:, c:c + 1]).then_inc(sem("c_v32"), 1)
                    act.activation(HI[:, side], bank((key, w)), ACT.Identity,
                                   bias=BQK[:, c:c + 1]).then_inc(sem("c_high"), 1)

            def out_copy(w):
                full(act, ("cV4", w))
                if w >= 2:
                    full(act, ("cA", w - 2))
                act.copy(AOS[:, w % 2], bank(("cV4", w))).then_inc(sem("c_aos"), 1)

            def back(w):
                b, g = divmod(w, GROUPS)
                if g == GROUPS - 1:
                    full(act, ("cT", b))
                    act.copy(AOT[0:64, :], bank(("cT", b))[0:64, :]).then_inc(sem("c_aot"), 1)
                    full(act, ("cO", b))
                    c = NCOL["L0_ffn_o_b"]
                    act.activation(XT[:, b], bank(("cO", b)), ACT.Identity, bias=BN[:, c:c + 1]).then_inc(sem("c_mla"), 1)

            act.wait_ge(sem("expand_cols"), 1)
            prepare(0)
            prepare(1)
            for w in range(last + 1):
                for i in range(8):
                    n = 8 * w + i
                    full(act, ("cP", w, i))
                    if n >= PT_SLOTS:
                        full(act, ("cV4", (n - PT_SLOTS) // 8))
                    act.activation(PT[:, n % PT_SLOTS], bank(("cP", w, i)), ACT.Exp, scale=0.5).then_inc(sem("c_exp"), 1)
                if w + 2 <= last:
                    prepare(w + 2)
                out_copy(w)
                if w:
                    back(w - 1)
            back(last)
            act.wait_ge(sem("r_shift"), 1)
            act.activation(RT[1], RT[0], ACT.Exp).then_inc(sem("r_exp"), 1)
            for b in range(B):
                full(act, ("rc", b))
                act.copy(CT[0:NE, b], bank(("rc", b))[0:NE, :]).then_inc(sem("r_ct"), 1)
            c0 = NCOL["L0_ffn_b1"]
            for i in range(B * NE):
                for c in range(2):
                    full(act, ("h1", i, c))
                    k = c0 + 2 * (i % NE) + c
                    act.activation(H1[:, i % 2, c], bank(("h1", i, c)), ACT.Gelu, bias=BN[:, k:k + 1]
                                   ).then_inc(sem("h1_ready"), 1)

        def vector_c(dve, link):
            last = B * GROUPS - 1
            dve.memset(WX, 0.0).then_inc(sem("c_init"), 1)
            dve.memset(VC, 0.0).then_inc(sem("c_init"), 1)
            dve.memset(AOT, 0.0).then_inc(sem("c_init"), 1)
            dve.memset(TMX, 0.0).then_inc(sem("c_init"), 1)
            dve.wait_ge(sem("c_init"), 4)
            dve.wait_ge(sem("cw_in"), 160)
            for side, src in enumerate((QW.rearrange("p (h c) -> p h c", c=HDC)[:, :, 0:KPH],
                                        KW.rearrange("p (h c) -> p h c", c=KPH))):
                dst = WX[:, side].rearrange("p g (j r) -> p (g j) r", r=32)[:, :, 0:6 * KPH]
                dve.tensor_copy(dst.rearrange("p h (t c) -> p h t c", c=KPH),
                                src.unsqueeze(2).to_broadcast([P, HC, 6, KPH])).then_inc(sem("expanded"), 1)
            link(dve.memset(VC.rearrange("p b k h e -> p (b k h) e")[:, :, KPH], 1.0))
            full(dve, ("tb", 2))
            dve.tensor_copy(BQK[:], bank(("tb", 2))[:, 0:2 * GROUPS]).then_inc(sem("expand_cols"), 1)

            def prepare(w):
                b, g = divmod(w, GROUPS)
                if g == 0:
                    full(dve, ("cV", b))
                    for kt in range(QT):
                        ins = dve.tensor_tensor(VC[:, b % 2, kt, :, 0:KPH],
                                                bank(("cV", b))[:, kt * 64:kt * 64 + 64].rearrange("p (h c) -> p h c", c=KPH),
                                                BVC.rearrange("p (h c) -> p h c", c=KPH), ALU.add)
                    ins.then_inc(sem("c_v"), 1)
                for side, name in enumerate("qk"):
                    dve.wait_ge(sem("c_high"), 2 * w + side + 1)
                    link(dve.scalar_tensor_tensor(out=R1[:, side], in0=HI[:, side], scalar=const(name + "_less_high"),
                                                  in1=V32[:, side], op0=ALU.mult, op1=ALU.add))
                    link(dve.tensor_copy(MID[:, side], R1[:, side]))
                    ins = dve.scalar_tensor_tensor(out=QS[:, w % 2] if side == 0 else KST, in0=MID[:, side],
                                                   scalar=const(name + "_less_mid"), in1=R1[:, side],
                                                   op0=ALU.mult, op1=ALU.add)
                    if side == 0:
                        ins.then_inc(sem("c_qs"), 1)
                    else:
                        link(ins)
                for j in range(4):
                    ins = dve.tensor_scalar(KM[:, w % 2, j], KST, const("head_rows")[:, j:j + 1], None, ALU.mult)
                ins.then_inc(sem("c_km"), 1)

            def maxima(w):
                for i in range(8):
                    t, jp = divmod(i, 2)
                    full(dve, ("cS", w, i))
                    dve.tensor_reduce(NMX[:, w % 2, t, 2 * jp:2 * jp + 2], bank(("cS", w, i)), AX.X, ALU.max,
                                      negate=True).then_inc(sem("c_max"), 1)

            def split_maxima(w):
                dve.wait_ge(sem("c_max"), 8 * w + 8)
                part = [TMX[:, w % 2].rearrange("p t (j r) -> p t j r", r=32)[:, :, :, 24 + k] for k in range(3)]
                link(dve.tensor_copy(part[0], NMX[:, w % 2]))
                link(dve.tensor_tensor(RMX, NMX[:, w % 2], part[0], ALU.subtract))
                link(dve.tensor_copy(part[1], RMX))
                dve.tensor_tensor(part[2], RMX, part[1], ALU.subtract).then_inc(sem("c_tmx"), 1)

            def add_maxima(w):
                full(dve, ("cM", w))
                dve.wait_ge(sem("c_qs"), w + 1)
                dve.tensor_tensor(QS[:, w % 2], QS[:, w % 2], bank(("cM", w)).bitcast(BF16)[:, 0:S],
                                  ALU.add).then_inc(sem("c_qm"), 1)

            def back(w):
                b, g = divmod(w, GROUPS)
                full(dve, ("cA", w))
                if w:
                    dve.wait_ge(sem("c_ao"), w)
                o = bank(("cA", w)).rearrange("p (t j r) -> p t j r", t=QT, j=4)
                link(dve.reciprocal(RCP, o[:, :, :, KPH]))
                for t in range(QT):
                    ins = dve.tensor_tensor(
                        AOTOK[:, b % 2, t, g * 16:g * 16 + 16].rearrange("p (j c) -> p j c", c=KPH), o[:, t, :, 0:KPH],
                        RCP[:, t, :].unsqueeze(2).to_broadcast([P, 4, KPH]), ALU.mult)
                ins.then_inc(sem("c_ao"), 1)

            prepare(0)
            maxima(0)
            split_maxima(0)
            prepare(1)
            add_maxima(0)
            for w in range(last + 1):
                if w < last:
                    maxima(w + 1)
                    split_maxima(w + 1)
                if w + 2 <= last:
                    prepare(w + 2)
                if w < last:
                    add_maxima(w + 1)
                if w:
                    back(w - 1)
            back(last)

            bc = lambda t: t.unsqueeze(2).to_broadcast([P, B * QT, NE])
            LG, PR, EQ, O1, P2, O2, SEL, WG, CMB = RT[0], RT[1], RT[2], RT[3], RT[4], RT[5], RT[6], RT[7], RT[11]
            full(dve, ("rt", 0))
            dve.tensor_tensor(RT[8], bank(("rt", 0))[:, 0:B * QT * NE].rearrange("p (n e) -> p n e", e=NE),
                              RB[:].unsqueeze(1).to_broadcast([P, B * QT, NE]), ALU.add).then_inc(sem("r_logits"), 1)
            dve.wait_ge(sem("r_logits"), 1)
            link(dve.tensor_reduce(RS1[0], RT[8], AX.X, ALU.max))
            dve.tensor_tensor(LG, RT[8], bc(RS1[0]), ALU.subtract).then_inc(sem("r_shift"), 1)
            dve.wait_ge(sem("r_exp"), 1)
            link(dve.tensor_reduce(RS1[1], PR, AX.X, ALU.add))
            link(dve.reciprocal(RS1[2], RS1[1]))
            link(dve.tensor_tensor(RT[9], PR, bc(RS1[2]), ALU.mult))
            turn = const("turn").unsqueeze(1).to_broadcast([P, B * QT, NE])

            def largest(p, one_hot):
                link(dve.tensor_reduce(RS1[3], p, AX.X, ALU.max))
                link(dve.tensor_tensor(EQ, p, bc(RS1[3]), ALU.is_equal))
                link(dve.tensor_tensor(RT[10], EQ, turn, ALU.mult))
                link(dve.tensor_reduce(RS1[4], RT[10], AX.X, ALU.max))
                link(dve.tensor_tensor(one_hot, RT[10], bc(RS1[4]), ALU.is_equal))

            largest(RT[9], O1)
            link(dve.scalar_tensor_tensor(out=P2, in0=O1, scalar=-2.0, in1=RT[9], op0=ALU.mult, op1=ALU.add))
            largest(P2, O2)
            link(dve.tensor_tensor(SEL, O1, O2, ALU.add))
            link(dve.tensor_tensor(WG, SEL, RT[9], ALU.mult))
            link(dve.tensor_reduce(RS1[5], WG, AX.X, ALU.add))
            link(dve.tensor_scalar(RS1[6], RS1[5], 1e-8, None, ALU.add))
            link(dve.reciprocal(RS1[7], RS1[6]))
            dve.tensor_tensor(CMB, WG, bc(RS1[7]), ALU.mult).then_inc(sem("r_comb"), 1)
            dve.wait_ge(sem("r_comb"), 1)

            for i in range(B * NE):
                b, e = divmod(i, NE)
                if e == 0:
                    full(dve, ("b2", b))
                    if b >= 2:
                        dve.wait_ge(sem("x_new"), 2 * B + b - 1)
                    dve.tensor_copy(ACC[:, b % 2], bank(("b2", b))).then_inc(sem("acc_set"), 1)
                full(dve, ("h2", i))
                if i >= 2:
                    dve.wait_ge(sem("summed"), i - 1)
                dve.tensor_tensor(TMP[:, i % 2].rearrange("p (t d) -> p t d", t=QT),
                                  bank(("h2", i)).rearrange("p (t d) -> p t d", t=QT),
                                  CMB[:, b * QT:(b + 1) * QT, e].unsqueeze(2).to_broadcast([P, QT, P]),
                                  ALU.mult).then_inc(sem("weighed"), 1)
                if e == NE - 1:
                    dve.wait_ge(sem("summed"), i + 1)
                    dve.wait_ge(sem("xy"), b + 1)
                    dve.scalar_tensor_tensor(out=X[:, b], in0=ACC[:, b % 2].rearrange("p (t d) -> p t d", t=QT),
                                             scalar=0.3, in1=X[:, b], op0=ALU.mult, op1=ALU.add).then_inc(sem("x_new"), 1)

        def pool_c(pool):
            for b in range(B):
                pool.wait_ge(sem("ln_y"), 2 * B + b + 1)
                pool.tensor_tensor(X[:, b], X[:, b], Y[:, b], ALU.add).then_inc(sem("xy"), 1)
            for i in range(B * NE):
                b = i // NE
                pool.wait_ge(sem("weighed"), i + 1)
                pool.wait_ge(sem("acc_set"), b + 1)
                if i:
                    pool.wait_ge(sem("summed"), i)
                pool.tensor_tensor(ACC[:, b % 2], ACC[:, b % 2], TMP[:, i % 2], ALU.add).then_inc(sem("summed"), 1)

        STEPS1 = B * len(TILES1)
        SCALE1 = float(P ** -0.5)

        def tensor_d(pe, begin, done, ln_turn):
            pe.wait_ge(sem("d_weights_in"), 80)
            for i in range(4):
                m, half = divmod(i, 2)
                o = begin(("gt", i))
                if i == 0:
                    pe.wait_ge(sem("x_new"), 3 * B)
                for c in range(4):
                    k = (4 * half + c) * P
                    mm = pe.transpose(o[:, c * P:(c + 1) * P], WQK1[m][:, k:k + P], ident)
                done(mm, ("gt", i))
            for m in range(2):
                pe.wait_ge(sem("gram_turned"), 2 * m + 2)
                o = begin(("gg", m))
                for c in range(8):
                    mm = pe.matmul(o[:, 0:P], WT[m][:, c, :], WT[m][:, c, :], start=c == 0, stop=c == 7)
                done(mm, ("gg", m))
            for b in range(B):
                ln_turn(3, b)
            pe.wait_ge(sem("gram"), 2)
            for b in range(B):
                pe.wait_ge(sem("xt_ready"), 3 * B + b + 1)
                for m in range(2):
                    o = begin(("z", b, m))
                    for t in range(QT):
                        mm = pe.matmul(o[:, t * P:(t + 1) * P], XT[:, b, t * P:(t + 1) * P], GM[:, m, :], start=True, stop=True)
                    done(mm, ("z", b, m))

            def turn_y(b):
                for m in range(2):
                    pe.wait_ge(sem("ym"), 2 * b + m + 1)
                    o = begin(("yt", b, m))
                    for t in range(QT):
                        mm = pe.transpose(o[:, t * P:(t + 1) * P], YM[:, m, t, :], ident)
                    done(mm, ("yt", b, m))

            def start(n):
                b, ti = divmod(n, len(TILES1))
                q0, nq, k0, _ = TILES1[ti]
                if ti == 0:
                    pe.wait_ge(sem("xqk"), 2 * b + 2)
                    for h in range(HD1):
                        for m, key in enumerate(("dQ", "dK")):
                            o = begin((key, b, h))
                            done(pe.matmul(o, WQK1[m][:, h * P:(h + 1) * P], XQK[:, b % 2, m], start=True, stop=True),
                                 (key, b, h))
                    if b + 1 < B:
                        turn_y(b + 1)
                    pe.wait_ge(sem("d_q"), HD1 * (b + 1))
                    pe.wait_ge(sem("d_k"), HD1 * (b + 1))
                o = begin(("dS", n)).rearrange("p k (h c) -> p (k h) c", c=P)
                for h in range(HD1):
                    mm = pe.matmul(o[0:nq, h, :], QT1[:, h, q0:q0 + nq], KT1[:, h, k0:k0 + P], start=True, stop=True)
                done(mm, ("dS", n))
                o = begin(("dV", n))
                for half in range(2):
                    mm = pe.matmul(o[:, half, :], XT[:, b, k0:k0 + P], WV1[:, half * 512:(half + 1) * 512],
                                   start=True, stop=True)
                done(mm, ("dV", n))

            def finish(n):
                b, ti = divmod(n, len(TILES1))
                q0, nq, k0, _ = TILES1[ti]
                pe.wait_ge(sem("d_pt"), n + 1)
                pe.wait_ge(sem("d_v"), n + 1)
                o = begin(("dY", n)).rearrange("p k (h c) -> p (k h) c", c=P)
                for h in range(HD1):
                    mm = pe.matmul(o[:, h, 0:nq], V1[:, n % 4, h * P:(h + 1) * P], PT1[:, n % 2, h, 0:nq],
                                   start=True, stop=True)
                done(mm, ("dY", n))
                if ti == len(TILES1) - 1:
                    pe.wait_ge(sem("d_y"), n + 1)
                    o = begin(("out1", b))
                    for t in range(QT):
                        for h in range(HD1):
                            mm = pe.matmul(o[:, t * P:(t + 1) * P], YT1[:, h, t * P:(t + 1) * P], WO1[:, h, :],
                                           start=h == 0, stop=h == HD1 - 1)
                    done(mm, ("out1", b))

            turn_y(0)
            start(0)
            start(1)
            for n in range(STEPS1):
                if n + 2 < STEPS1:
                    start(n + 2)
                if n:
                    finish(n - 1)
                nq = TILES1[n % len(TILES1)][1]
                pe.wait_ge(sem("d_norm"), n + 1)
                o = begin(("dT", n)).rearrange("p k (h c) -> p (k h) c", c=P)
                for h in range(HD1):
                    mm = pe.transpose(o[:, h, 0:nq], SM[0:nq, n % 3, h, :], ident[0:nq, 0:nq])
                done(mm, ("dT", n))
            finish(STEPS1 - 1)

        def scalar_d(act, rstd, xt_out):
            for i in range(4):
                m, half = divmod(i, 2)
                full(act, ("gt", i))
                act.copy(WT[m][:, 4 * half:4 * half + 4, :].rearrange("p c d -> p (c d)"), bank(("gt", i))
                         ).then_inc(sem("gram_turned"), 1)
            for m in range(2):
                full(act, ("gg", m))
                act.copy(GM[:, m, :], bank(("gg", m))[:, 0:P]).then_inc(sem("gram"), 1)
            act.preload_act_table_set("natural_log_exp_and_others")
            for b in range(B):
                rstd(3, b)
            for b in range(B):
                xt_out(3, b)
            for b in range(B):
                act.wait_ge(sem("ss"), b + 1)
                act.activation(RL[:, b], SS[:, b], ACT.Ln, scale=1.0 / (HD1 * P), bias=const("eps_rms")
                               ).then_inc(sem("r_log"), 1)
                act.wait_ge(sem("r_log"), b + 1)
                act.activation(RMS[:, b], RL[:, b], ACT.Exp, scale=-0.5).then_inc(sem("r_rms"), 1)

            def turn_y(b):
                for m in range(2):
                    full(act, ("yt", b, m))
                    act.copy(XQK[:, b % 2, m], bank(("yt", b, m))).then_inc(sem("xqk"), 1)

            def start(n):
                b, ti = divmod(n, len(TILES1))
                if ti == 0:
                    for h in range(HD1):
                        full(act, ("dK", b, h))
                        c = NCOL["L1_attn_k_norm_w"] + h
                        act.activation(KT1[:, h], bank(("dK", b, h)), ACT.Copy, scale=BN[:, c:c + 1]).then_inc(sem("d_k"), 1)
                    if b + 1 < B:
                        turn_y(b + 1)

            def softmax(n):
                nq = TILES1[n % len(TILES1)][1]
                act.wait_ge(sem("d_max"), n + 1)
                for h in range(HD1):
                    act.activation(SM[0:nq, n % 3, h], SM[0:nq, n % 3, h], ACT.Exp, bias=NM1[0:nq, n % 3, h:h + 1],
                                   accum_out=SUM1[0:nq, n % 3, h:h + 1]).then_inc(sem("d_exp"), 1)

            def turned(n):
                nq = TILES1[n % len(TILES1)][1]
                full(act, ("dT", n))
                act.copy(PT1[:, n % 2, :, 0:nq], bank(("dT", n)).rearrange("p k (h c) -> p (k h) c", c=P)[:, :, 0:nq]
                         ).then_inc(sem("d_pt"), 1)

            turn_y(0)
            start(0)
            start(1)
            for n in range(STEPS1):
                early = n > 0 and (n + 2) % len(TILES1) == 0
                if early:
                    turned(n - 1)
                if n + 2 < STEPS1:
                    start(n + 2)
                softmax(n)
                if n and not early:
                    turned(n - 1)
            turned(STEPS1 - 1)

        def vector_d(dve, link, layernorm, add_to_stream):
            layernorm(3)
            for b in range(B):
                for m in range(2):
                    full(dve, ("z", b, m))
                    if b:
                        dve.wait_ge(sem("ss"), b)
                    dve.tensor_tensor(ZY[:, m], Y[:, b], bank(("z", b, m)).rearrange("p (t d) -> p t d", t=QT),
                                      ALU.mult).then_inc(sem("zy"), 1)
                dve.wait_ge(sem("zy"), 2 * b + 2)
                dve.tensor_reduce(SS[:, b], ZY, AX.X, ALU.add).then_inc(sem("ss"), 1)

            def scale_y(b):
                dve.wait_ge(sem("r_rms"), b + 1)
                for m in range(2):
                    if b:
                        full(dve, ("yt", b - 1, m))
                    else:
                        dve.wait_ge(sem("ss"), B)
                    dve.tensor_tensor(YM[:, m], Y[:, b], RMS[:, b, m].unsqueeze(2).to_broadcast([P, QT, P]),
                                      ALU.mult).then_inc(sem("ym"), 1)

            def start(n):
                b, ti = divmod(n, len(TILES1))
                if ti == 0:
                    if b + 1 < B:
                        scale_y(b + 1)
                    for h in range(HD1):
                        full(dve, ("dQ", b, h))
                        c = NCOL["L1_attn_q_norm_w"] + h
                        dve.tensor_scalar(QT1[:, h], bank(("dQ", b, h)), BN[:, c:c + 1], None, ALU.mult).then_inc(sem("d_q"), 1)
                nq, kind = TILES1[ti][1], TILES1[ti][3]
                full(dve, ("dS", n))
                if n == 0:
                    dve.wait_ge(sem("bias_in"), 16)
                if n >= 3:
                    full(dve, ("dT", n - 3))
                dve.scalar_tensor_tensor(out=SM[0:nq, n % 3].rearrange("p h c -> p (h c)"),
                                         in0=bank(("dS", n))[0:nq].rearrange("p k c -> p (k c)"), scalar=SCALE1,
                                         in1=BM[0:nq, kind].rearrange("p h c -> p (h c)"),
                                         op0=ALU.mult, op1=ALU.add).then_inc(sem("d_biased"), 1)
                dve.wait_ge(sem("d_biased"), n + 1)
                dve.tensor_reduce(NM1[0:nq, n % 3], SM[0:nq, n % 3], AX.X, ALU.max, negate=True).then_inc(sem("d_max"), 1)
                full(dve, ("dV", n))
                if n >= 4:
                    full(dve, ("dY", n - 4))
                dve.tensor_copy(V1[:, n % 4], bank(("dV", n)).rearrange("p k c -> p (k c)")).then_inc(sem("d_v"), 1)

            def finish(n):
                b, ti = divmod(n, len(TILES1))
                q0, nq = TILES1[ti][0:2]
                full(dve, ("dY", n))
                dve.tensor_copy(YT1[:, :, q0:q0 + nq], bank(("dY", n)).rearrange("p k (h c) -> p (k h) c", c=P)[:, :, 0:nq]
                                ).then_inc(sem("d_y"), 1)
                if ti == len(TILES1) - 1:
                    add_to_stream(3, b, ("out1", b))

            def weights(n):
                nq = TILES1[n % len(TILES1)][1]
                dve.wait_ge(sem("d_exp"), HD1 * (n + 1))
                link(dve.reciprocal(RC1[0:nq, n % 3], SUM1[0:nq, n % 3]))
                dve.tensor_tensor(SM[0:nq, n % 3], SM[0:nq, n % 3],
                                  RC1[0:nq, n % 3].unsqueeze(2).to_broadcast([nq, HD1, P]), ALU.mult).then_inc(sem("d_norm"), 1)

            scale_y(0)
            start(0)
            start(1)
            for n in range(STEPS1):
                if n + 2 < STEPS1:
                    start(n + 2)
                if n:
                    finish(n - 1)
                weights(n)
            finish(STEPS1 - 1)

        STEPS = B * QT
        SCALEX = float(DX ** -0.5)

        def tensor_e(pe, begin, done, ln_turn):
            pe.wait_ge(sem("e_weights_in"), 16 * 13)
            o = begin(("eK", 0))
            done(pe.matmul(o[:, 0:P], EW["k"], CTXT[:], start=True, stop=True), ("eK", 0))
            pe.wait_ge(sem("e_ctx4"), 1)
            for b in range(B):
                o = begin(("eV", b))
                done(pe.matmul(o[:, 0:P], CT4[:, b], EW["v"], start=True, stop=True), ("eV", b))
            for b in range(B):
                ln_turn(4, b)
            for b in range(B):
                pe.wait_ge(sem("xt_ready"), 4 * B + b + 1)
                o = begin(("eQ", b))
                done(pe.matmul(o, EW["q"], XT[:, b], start=True, stop=True), ("eQ", b))

            def scores(n):
                b, t = divmod(n, QT)
                pe.wait_ge(sem("e_q"), b + 1)
                pe.wait_ge(sem("e_kx"), b + 1)
                o = begin(("eS", n))
                done(pe.matmul(o, QTX[:, b, t * P:(t + 1) * P], KX[:, b].rearrange("p h j -> p (h j)"), start=True, stop=True),
                     ("eS", n))

            scores(0)
            scores(1)
            for n in range(STEPS):
                b, t = divmod(n, QT)
                if n + 2 < STEPS:
                    scores(n + 2)
                pe.wait_ge(sem("e_p"), n + 1)
                o = begin(("eT", n))
                p = PE1[:, n % 3].rearrange("p h j -> p (h j)")
                for g in range(4):
                    mm = pe.transpose(o[:, g * P:(g + 1) * P], p[:, g * P:(g + 1) * P], ident)
                done(mm, ("eT", n))
                if t == QT - 1:
                    pe.wait_ge(sem("e_pt"), n + 1)
                    pe.wait_ge(sem("e_vx"), b + 1)
                    o = begin(("eO", b))
                    for g in range(4):
                        mm = pe.matmul(o, VX[:, b, g, :], PTE[:, b % 2, g, :], start=g == 0, stop=g == 3)
                    done(mm, ("eO", b))
                    pe.wait_ge(sem("e_o"), b + 1)
                    o = begin(("eX", b))
                    for k in range(QT):
                        mm = pe.matmul(o[:, k * P:(k + 1) * P], OTE[:, b % 2, k * P:(k + 1) * P], EW["out"], start=True, stop=True)
                    done(mm, ("eX", b))

        def scalar_e(act, rstd, xt_out):
            full(act, ("eK", 0))
            act.wait_ge(sem("x_new"), 4 * B)
            c = NCOL["L1_xattn_bkv"]
            act.activation(KTX.rearrange("p b j -> p (b j)"), bank(("eK", 0))[:, 0:P], ACT.Identity,
                           bias=BN[:, c:c + 1]).then_inc(sem("e_k"), 1)
            for b in range(B):
                rstd(4, b)
            for b in range(B):
                xt_out(4, b)
            c = NCOL["L1_xattn_bq"]
            for b in range(B):
                full(act, ("eQ", b))
                act.activation(QTX[:, b], bank(("eQ", b)), ACT.Identity, bias=BN[:, c:c + 1]).then_inc(sem("e_q"), 1)

            def turned(n):
                b, t = divmod(n, QT)
                full(act, ("eT", n))
                act.copy(PTE[:, b % 2, :, t * P:(t + 1) * P], bank(("eT", n)).rearrange("p (g q) -> p g q", g=4)
                         ).then_inc(sem("e_pt"), 1)
                if t == QT - 1:
                    full(act, ("eO", b))
                    act.copy(OTE[:, b % 2], bank(("eO", b))).then_inc(sem("e_o"), 1)

            for n in range(STEPS):
                act.wait_ge(sem("e_shift"), n + 1)
                if n >= 3:
                    full(act, ("eT", n - 3))
                act.activation(PE1[:, n % 3], SE[:, n % 3], ACT.Exp).then_inc(sem("e_exp"), 1)
                if n:
                    turned(n - 1)
            turned(STEPS - 1)

        def vector_e(dve, link, layernorm, add_to_stream):
            dve.wait_ge(sem("x_new"), 4 * B)
            link(dve.tensor_copy(MB[:].rearrange("p b j -> p (b j)"), MK8[:]))
            dve.tensor_scalar(MB[:], MB[:], -3e38, 10.0, ALU.mult, ALU.mult).then_inc(sem("mask_bias"), 1)
            dve.tensor_copy(CT4.rearrange("p b (r j) -> p b r j", r=4),
                            CTXT[:].rearrange("p (b j) -> p b j", b=B).unsqueeze(2).to_broadcast([P, B, 4, CK])
                            ).then_inc(sem("e_ctx4"), 1)
            dve.wait_ge(sem("e_k"), 1)
            for b in range(B):
                dve.tensor_tensor(KX[:, b], KTX[:, b].unsqueeze(1).to_broadcast([P, HX, CK]),
                                  const("xhead").unsqueeze(2).to_broadcast([P, HX, CK]), ALU.mult).then_inc(sem("e_kx"), 1)
            for b in range(B):
                full(dve, ("eV", b))
                if b >= 2:
                    dve.wait_ge(sem("e_vx"), b - 1)
                dve.tensor_tensor(V4[:, b % 2], bank(("eV", b))[:, 0:P], EW["bias_v"], ALU.add).then_inc(sem("e_v4"), 1)
                dve.wait_ge(sem("e_v4"), b + 1)
                dve.tensor_tensor(VX[:, b], V4[:, b % 2].unsqueeze(1).to_broadcast([P, 4, P]),
                                  const("vhead").rearrange("p (g c) -> p g c", g=4), ALU.mult).then_inc(sem("e_vx"), 1)
            layernorm(4)
            dve.wait_ge(sem("mask_bias"), 1)

            def sums(n):
                dve.wait_ge(sem("e_exp"), n + 1)
                if n >= 2:
                    dve.wait_ge(sem("e_p"), n - 1)
                link(dve.tensor_reduce(SUE[:, n % 2], PE1[:, n % 3], AX.X, ALU.add))
                dve.reciprocal(RCE[:, n % 2], SUE[:, n % 2]).then_inc(sem("e_rc"), 1)

            for n in range(STEPS):
                b, t = divmod(n, QT)
                full(dve, ("eS", n))
                if n >= 3:
                    dve.wait_ge(sem("e_exp"), n - 2)
                if n >= 2:
                    dve.wait_ge(sem("e_shift"), n - 1)
                dve.scalar_tensor_tensor(out=SE[:, n % 3], in0=bank(("eS", n)).rearrange("p (h j) -> p h j", h=HX),
                                         scalar=SCALEX, in1=MB[:, b].unsqueeze(1).to_broadcast([P, HX, CK]),
                                         op0=ALU.mult, op1=ALU.add).then_inc(sem("e_biased"), 1)
                dve.wait_ge(sem("e_biased"), n + 1)
                link(dve.tensor_reduce(NME[:, n % 2], SE[:, n % 3], AX.X, ALU.max))
                dve.tensor_tensor(SE[:, n % 3], SE[:, n % 3], NME[:, n % 2].unsqueeze(2).to_broadcast([P, HX, CK]),
                                  ALU.subtract).then_inc(sem("e_shift"), 1)
                if n:
                    sums(n - 1)
                if n >= QT + 1 and (n - 1) % QT == 0:
                    pb = (n - 1) // QT - 1
                    if pb == 0:
                        dve.wait_ge(sem("xb4"), B)
                    add_to_stream(4, pb, ("eX", pb))
            sums(STEPS - 1)
            add_to_stream(4, B - 1, ("eX", B - 1))

        def pool_e(pool):
            pool.wait_ge(sem("e_weights_in"), 16 * 13)
            for b in range(B):
                pool.wait_ge(sem("ln_y"), 4 * B + b + 1)
                pool.tensor_tensor(X[:, b], X[:, b], EW["bias_out"].unsqueeze(1).to_broadcast([P, QT, P]),
                                   ALU.add).then_inc(sem("xb4"), 1)
            for n in range(STEPS):
                pool.wait_ge(sem("e_rc"), n + 1)
                pool.tensor_tensor(PE1[:, n % 3], PE1[:, n % 3], RCE[:, n % 2].unsqueeze(2).to_broadcast([P, HX, CK]),
                                   ALU.mult).then_inc(sem("e_p"), 1)

        def quantize(dve, link, rows, src, n, dst, name):
            blocks = n // BLK
            r = slice(0, rows)
            amax, sc, rc, half = (QSC[r, k, 0:blocks] for k in range(4))
            by = lambda t: t[r, 0:n].rearrange("p (k i) -> p k i", i=BLK)
            wide = lambda t: t.unsqueeze(2).to_broadcast([rows, blocks, BLK])
            v = src.rearrange("p (k i) -> p k i", i=BLK)
            link(dve.tensor_reduce(amax, v, AX.X, ALU.max, apply_absolute_value=True))
            link(dve.tensor_scalar(sc, amax, float(np.float32(1 / 6)), 1e-12, ALU.mult, ALU.max))
            link(dve.reciprocal(rc, sc))
            dve.tensor_scalar(half, sc, 0.5, None, ALU.mult)
            link(dve.tensor_tensor(by(QA_), v, wide(rc), ALU.mult))
            A, U, W = QA_[r, 0:n], QB_[r, 0:n], QC_[r, 0:n]
            M = QD_[r, 0:n]
            link(dve.tensor_scalar(M.bitcast(U32), A.bitcast(U32), 0x7FFFFFFF, None, ALU.bitwise_and))
            dve.tensor_scalar(U, M, 0.25, None, ALU.is_gt)
            link(dve.tensor_scalar(W, M, 5.0, 2.0, ALU.is_gt, ALU.mult))
            for lo, hi in ((0.75, 3.5), (1.25, 2.5)):
                dve.scalar_tensor_tensor(out=U, in0=M, scalar=lo, in1=U, op0=ALU.is_gt, op1=ALU.add)
                link(dve.scalar_tensor_tensor(out=W, in0=M, scalar=hi, in1=W, op0=ALU.is_gt, op1=ALU.add))
            link(dve.scalar_tensor_tensor(out=U, in0=M, scalar=1.75, in1=U, op0=ALU.is_gt, op1=ALU.add))
            link(dve.scalar_tensor_tensor(out=U, in0=W, scalar=2.0, in1=U, op0=ALU.mult, op1=ALU.add))
            link(dve.scalar_tensor_tensor(out=W.bitcast(U32), in0=A.bitcast(U32), scalar=SIGN[r, :], in1=U.bitcast(U32),
                                          op0=ALU.bitwise_and, op1=ALU.bitwise_or))
            dve.tensor_tensor(dst.rearrange("p (k i) -> p k i", i=BLK), by(QC_), wide(half), ALU.mult
                              ).then_inc(sem(name), 1)
            return dve

        def tensor_f(pe, begin, done):
            pe.wait_ge(sem("f_wq"), 7)
            for i in range(3):
                o = begin(("fW", i))
                for c, (r0, n) in enumerate(FCH):
                    if i < 2:
                        mm = pe.transpose(o[:, r0:r0 + n], WQT[0:n, i, c * P:(c + 1) * P], ident[0:n, 0:n])
                    else:
                        mm = pe.transpose(o[0:n, c * P:(c + 1) * P], WQT[:, 2, r0:r0 + n], ident)
                done(mm, ("fW", i))
            for b in range(B):
                pe.wait_ge(sem("f_yq"), b + 1)
                o = begin(("fX", b))
                for t in range(QT):
                    mm = pe.transpose(o[:, t * P:(t + 1) * P], YQ[:, b % 2, t, :], ident)
                done(mm, ("fX", b))
            pe.wait_ge(sem("f_w"), 3)

            def start(n):
                b, t = divmod(n, QT)
                pe.wait_ge(sem("f_x"), b + 1)
                for i, key in enumerate(("fG", "fU")):
                    o = begin((key, n))
                    done(pe.matmul(o[:, 0:FI], XQT[:, b, t * P:(t + 1) * P], WGU[:, i, :], start=True, stop=True), (key, n))

            def down(n):
                pe.wait_ge(sem("f_ht"), n + 1)
                o = begin(("fD", n))
                for c, (r0, k) in enumerate(FCH):
                    mm = pe.matmul(o[:, 0:P], HQT[0:k, n % 2, c, :], WD[0:k, c, :], start=c == 0, stop=c == 2)
                done(mm, ("fD", n))

            start(0)
            start(1)
            for n in range(STEPS):
                if n + 2 < STEPS:
                    start(n + 2)
                if n:
                    down(n - 1)
                pe.wait_ge(sem("f_hq"), n + 1)
                o = begin(("fT", n))
                for c, (r0, k) in enumerate(FCH):
                    mm = pe.transpose(o[0:k, c * P:(c + 1) * P], HQ[:, n % 2, r0:r0 + k], ident)
                done(mm, ("fT", n))
            down(STEPS - 1)

        def scalar_f(act, rstd):
            for i in range(2):
                full(act, ("fW", i))
                act.copy(WGU[:, i, :], bank(("fW", i))[:, 0:FI]).then_inc(sem("f_w"), 1)
            full(act, ("fW", 2))
            act.copy(WD[:, 0:2, :].rearrange("p c d -> p (c d)"), bank(("fW", 2))[:, 0:2 * P])
            act.copy(WD[0:96, 2, :], bank(("fW", 2))[0:96, 2 * P:3 * P]).then_inc(sem("f_w"), 1)
            for b in range(B):
                rstd(5, b)
            for b in range(B):
                full(act, ("fX", b))
                act.copy(XQT[:, b], bank(("fX", b))).then_inc(sem("f_x"), 1)

            def silu(n):
                full(act, ("fG", n))
                if n >= 3:
                    act.wait_ge(sem("f_h"), n - 2)
                act.activation(SG[:, n % 3], bank(("fG", n))[:, 0:FI], ACT.Silu).then_inc(sem("f_silu"), 1)

            def turned(n):
                full(act, ("fT", n))
                if n >= 2:
                    full(act, ("fD", n - 2))
                act.copy(HQT[:, n % 2, 0:2, :].rearrange("p c d -> p (c d)"), bank(("fT", n))[:, 0:2 * P])
                act.copy(HQT[0:96, n % 2, 2, :], bank(("fT", n))[0:96, 2 * P:3 * P]).then_inc(sem("f_ht"), 1)

            silu(0)
            silu(1)
            for n in range(STEPS):
                if n + 2 < STEPS:
                    silu(n + 2)
                turned(n)

        def vector_f(dve, link, stats, normalize):
            link(dve.memset(SIGN[:], 0x80000000))
            k = 0
            for i, name in enumerate(("gate", "up")):
                for c, (r0, n) in enumerate(FCH):
                    if k:
                        dve.wait_ge(sem("f_wq"), k)
                    quantize(dve, link, n, FW[name][0:n, c * P:(c + 1) * P], P, WQT[0:n, i, c * P:(c + 1) * P], "f_wq")
                    k += 1
            dve.wait_ge(sem("f_wq"), 6)
            quantize(dve, link, P, FW["down"], FI, WQT[:, 2, 0:FI], "f_wq")
            dve.wait_ge(sem("f_wq"), 7)
            for b in range(B):
                stats(5, b)
                if b:
                    normalize(5, b - 1)
            normalize(5, B - 1)
            dve.wait_ge(sem("ln_y"), 6 * B)
            for b in range(B):
                if b:
                    dve.wait_ge(sem("f_yq"), b)
                if b >= 2:
                    full(dve, ("fX", b - 2))
                quantize(dve, link, P, Y[:, b].rearrange("p t d -> p (t d)"), S, YQ[:, b % 2].rearrange("p t d -> p (t d)"), "f_yq")
            dve.wait_ge(sem("f_yq"), B)

            def add(n):
                b, t = divmod(n, QT)
                full(dve, ("fD", n))
                dve.tensor_tensor(X[:, b, t], X[:, b, t], bank(("fD", n))[:, 0:P], ALU.add).then_inc(sem("x_final"), 1)

            for n in range(STEPS):
                dve.wait_ge(sem("f_silu"), n + 1)
                full(dve, ("fU", n))
                if n:
                    dve.wait_ge(sem("f_hq"), n)
                dve.tensor_tensor(HF, SG[:, n % 3], bank(("fU", n))[:, 0:FI], ALU.mult).then_inc(sem("f_h"), 1)
                dve.wait_ge(sem("f_h"), n + 1)
                if n >= 2:
                    full(dve, ("fT", n - 2))
                quantize(dve, link, P, HF, FI, HQ[:, n % 2], "f_hq")
                if n:
                    add(n - 1)
            add(STEPS - 1)

        @block.sync
        def _(sp):
            sp.dma_start(C[:], a["consts"]).then_inc(sem("consts_in"), 16)
            for b in range(B):
                sp.dma_start(X[:, b], a["x"][b].rearrange("(t p) d -> p t d", p=P)).then_inc(sem("x_in"), 16)
            w_in = a["L0_attn_W_in"].rearrange("d (h k e) -> d k h e", k=4, e=E0)
            for half in range(2):
                sp.dma_start(WQ[:, :, half, :], w_in[:, 0]).then_inc(sem("win_in"), 16)
            for kind in range(3):
                sp.dma_start(WKVG[:, kind], w_in[:, kind + 1]).then_inc(sem("win_in"), 16)
            b_in = a["L0_attn_b_in"].rearrange("(r e) -> r e", e=E0)
            for half in range(2):
                sp.dma_start(BROW[:, half * 64:half * 64 + 64], b_in).then_inc(sem("rows_in"), 16)
            for name in NCOL:
                src = a[name]
                src = src.rearrange("e (c f) -> (e c) f", f=P) if name == "L0_ffn_b1" else src.rearrange("(r f) -> r f", f=P)
                sp.dma_start(NROW[NCOL[name]:NCOL[name] + src.shape[0], :], src).then_inc(sem("rows_in"), 16)
            sp.dma_start(BV[:], a["L0_attn_b_in"].rearrange("(h k e) -> h k e", k=4, e=E0)[:, 2, :]
                         .partition_broadcast(P)).then_inc(sem("bcast_in"), 16)
            sp.dma_start(Bout[:], a["L0_attn_b_out"].partition_broadcast(P)).then_inc(sem("bcast_in"), 16)
            sp.dma_start(Wout[:], a["L0_attn_W_out"].rearrange("(c p) d -> p c d", p=P)).then_inc(sem("bcast_in"), 16)
            for i, name in enumerate(("kernel_q", "kernel_k", "kernel_v")):
                sp.dma_start(XK[:, i, :], a["L0_xattn_" + name][0, 0]).then_inc(sem("xw_in"), 16)
            sp.dma_start(BXV[:], a["L0_xattn_bias_v"].partition_broadcast(P)).then_inc(sem("xw_in"), 16)
            sp.dma_start(CTX[:], a["ctx_1024"].rearrange("b s d -> (b s) d")).then_inc(sem("xw_in"), 16)
            for b in range(B):
                sp.dma_start(MSK[:, :, b * CK:(b + 1) * CK],
                             a["mask_1xSxS2_ff0"][0].rearrange("(t p) s -> p t s", p=P)).then_inc(sem("xw_in"), 16)
            for t, src in ((QW, a["L0_ffn_q_w"]), (KW, a["L0_ffn_k_w"]), (VW, a["L0_ffn_v_w"]), (OW, a["L0_ffn_o_w"]),
                           (RW, a["L0_ffn_router_w"]), (RB, a["L0_ffn_router_b"].partition_broadcast(P)),
                           (BVC, a["L0_ffn_v_b"].partition_broadcast(P)), (B2, a["L0_ffn_b2"]),
                           (W1, a["L0_ffn_w1"].rearrange("e d f -> d e f")),
                           (W2, a["L0_ffn_w2"].rearrange("e (c f) d -> f e c d", f=P))):
                sp.dma_start(t[:], src).then_inc(sem("cw_in"), 16)
            sp.wait_ge(sem("row_set"), 2)
            for t in range(6):
                for side, src in enumerate((a["L0_ffn_q_b"].rearrange("(o g j c) -> o g j c", o=1, g=GROUPS, j=4)[:, :, :, 0:KPH],
                                            a["L0_ffn_k_b"].rearrange("(o g j c) -> o g j c", o=1, g=GROUPS, j=4))):
                    for g in range(GROUPS):
                        dst = QKROW[:, side * GROUPS + g, :].rearrange("o (j r) -> o j r", j=4)[:, :, t * KPH:(t + 1) * KPH]
                        sp.dma_start(dst, src[:, g]).then_inc(sem("expand_rows_in"), 16)
            if stop > 3:
                sp.wait_ge(sem("g_sb"), UNITS)
                for t, src in ((WQK1[0], a["L1_attn_wq"]), (WQK1[1], a["L1_attn_wk"]), (WV1, a["L1_attn_wv"]),
                               (WO1, a["L1_attn_wo"].rearrange("(h p) d -> p h d", p=P))):
                    sp.dma_start(t, src).then_inc(sem("d_weights_in"), 16)
                sp.dma_start(MK8[:], a["mask_BxS2_bf0"].rearrange("b s -> (b s)").partition_broadcast(P)
                             ).then_inc(sem("d_weights_in"), 16)
                sp.wait_ge(sem("weighed"), B * NE)
                sp.wait_ge(sem("x_new"), 3 * B)
                sp.dma_start(BM, a["window_bias"].rearrange("p (k h c) -> p k h c", k=3, h=HD1)
                             ).then_inc(sem("bias_in"), 16)
                wkv = a["L1_xattn_Wkv"]
                for name, src in (("q", a["L1_xattn_Wq"]), ("k", wkv[:, 0:P]), ("v", wkv[:, P:2 * P]),
                                  ("out", a["L1_xattn_Wout"]), ("bias_v", a["L1_xattn_bkv"][P:2 * P].partition_broadcast(P)),
                                  ("bias_out", a["L1_xattn_bout"].partition_broadcast(P))):
                    sp.dma_start(EW[name], src).then_inc(sem("e_weights_in"), 16)
                for name in ("gate", "up"):
                    w = a["L1_ffn_w_" + name]
                    for c, (r0, n) in enumerate(FCH):
                        sp.dma_start(FW[name][0:n, c * P:(c + 1) * P], w[r0:r0 + n, :]).then_inc(sem("e_weights_in"), 16)
                sp.dma_start(FW["down"], a["L1_ffn_w_down"]).then_inc(sem("e_weights_in"), 16)
            if stop == 6:
                for b in range(B):
                    sp.wait_ge(sem("x_final"), QT * (b + 1))
                    sp.dma_start(out[b].rearrange("(t p) d -> p t d", p=P), X[:, b]).then_inc(sem("out_done"), 16)
                sp.wait_ge(sem("out_done"), 16 * B)
                return
            for b in range(B):
                sp.wait_ge(sem("x_new"), (stop - 1) * B + b + 1)
                sp.dma_start(out[b].rearrange("(t p) d -> p t d", p=P), X[:, b]).then_inc(sem("out_done"), 16)
            sp.wait_ge(sem("out_done"), 16 * B)
        LOADS_XW = 16 * 9

        @block.tensor
        def _(pe):
            order = iter(placed)

            def begin(key):
                assert next(order) == key, key
                for name, value in placed[key][3].items():
                    pe.wait_ge(sem(name), value)
                return bank(key)

            def done(mm, key):
                mm.then_inc(full_sem[placed[key][0]], 1)

            def transposes(key, src):
                o = begin(key)
                for t in range(QT):
                    mm = pe.transpose(o[:, t * P:(t + 1) * P], src[:, t, :], ident)
                done(mm, key)

            def ln_turn(k, b):
                pe.wait_ge(sem("ln_y"), k * B + b + 1)
                transposes(("ln", k, b), Y[:, b])

            def wpair(p, kind):
                return WKVG[:, kind, 2 * p:2 * p + 2, :].rearrange("p h e -> p (h e)")

            def project(u):
                b, p = divmod(u, PAIRS)
                for hd, key in ((0, "QA"), (1, "QB")):
                    o = begin((key, u))
                    w = WQ[:, 2 * p + hd].rearrange("p a e -> p (a e)")
                    done(pe.matmul(o, w, XT[:, b], start=True, stop=True), (key, u))
                o = begin(("K", u))
                done(pe.matmul(o, wpair(p, 0), XT[:, b], start=True, stop=True), ("K", u))
                o = begin(("V", u))
                for kt in range(QT):
                    mm = pe.matmul(o[:, kt * P:(kt + 1) * P], XT[:, b, kt * P:(kt + 1) * P], wpair(p, 1),
                                   start=True, stop=True)
                done(mm, ("V", u))
                o = begin(("G", u))
                done(pe.matmul(o, wpair(p, 2), XT[:, b], start=True, stop=True), ("G", u))

            def key_norms(u):
                o = begin(("k2", u))
                pe.wait_ge(sem("ksq"), 2 * u + 2)
                for kt in range(QT):
                    mm = pe.matmul(o[:, kt * P:(kt + 1) * P], KSQ[:, kt * P:(kt + 1) * P], const("pairsum"),
                                   start=True, stop=True)
                done(mm, ("k2", u))

            def scores(u):
                pe.wait_ge(sem("mq_scaled"), 2 * u + 2)
                pe.wait_ge(sem("mq_squared"), 2 * u + 2)
                pe.wait_ge(sem("k_sb"), 2 * u + 2)
                for c in range(8):
                    hd, kt = divmod(c, QT)
                    o = begin(("S", u, c))
                    done(pe.matmul(o, SK[:, hd, kt * P:(kt + 1) * P], MQ[:, hd, :], start=True, stop=True),
                         ("S", u, c))

            def weighted_values(u):
                pe.wait_ge(sem("w_ready"), 2 * u + 2)
                pe.wait_ge(sem("v_sb"), u + 1)
                for key in ("PV", "RS"):
                    o = begin((key, u))
                    for kt in range(QT):
                        for hd in range(2):
                            w = VA[:, u % 3, kt, hd * 64:hd * 64 + 64] if key == "PV" else const("ones")[:, 0:64]
                            mm = pe.matmul(o[hd * 64:hd * 64 + 64, :], w, D[:, u % 2, hd, kt, :],
                                           start=kt == 0, stop=kt == QT - 1)
                    done(mm, (key, u))

            def project_out(b):
                pe.wait_ge(sem("h_done"), (b + 1) * PAIRS)
                o = begin(("out0", b))
                for t in range(QT):
                    for p in range(PAIRS):
                        mm = pe.matmul(o[:, t * P:(t + 1) * P], HT[:, b % 2, p, t * P:(t + 1) * P], Wout[:, p, :],
                                       start=p == 0, stop=p == PAIRS - 1)
                done(mm, ("out0", b))

            pe.wait_ge(sem("consts_in"), 16)
            pe.wait_ge(sem("rows_in"), 16 * (2 + len(NCOL)))
            for i, rows in enumerate((BROW, NROW)):
                r = 64 if i == 0 else sum((1, 1, 1, 16, 8, 8, 1, 2))
                o = begin(("tb", i))
                done(pe.transpose(o[:, 0:r], rows[0:r, :], ident[0:r, 0:r]), ("tb", i))
            for b in range(B):
                ln_turn(0, b)
            pe.wait_ge(sem("win_in"), 16 * 5)
            pe.wait_ge(sem("xt_ready"), B)
            project(0)
            key_norms(0)
            for u in range(UNITS):
                scores(u)
                if u + 1 < UNITS:
                    project(u + 1)
                if u >= 1:
                    weighted_values(u - 1)
                if u + 1 < UNITS:
                    key_norms(u + 1)
                if u == 2:
                    pe.wait_ge(sem("bcast_in"), 48)
                if u >= 2 and (u - 2) % PAIRS == PAIRS - 1:
                    project_out((u - 2) // PAIRS)
            weighted_values(UNITS - 1)
            project_out(B - 1)

            pe.wait_ge(sem("xw_in"), LOADS_XW)
            transposes(("xmask", 0), MSK)
            o = begin(("ctxT", 0))
            done(pe.transpose(o[:, 0:P], CTX[:], ident), ("ctxT", 0))
            pe.wait_ge(sem("ctxT_sb"), 1)
            o = begin(("xk", 0))
            done(pe.matmul(o[:, 0:P], XK[:, 1, :], CTXT[:], start=True, stop=True), ("xk", 0))
            o = begin(("xv", 0))
            done(pe.matmul(o[:, 0:P], CTXT[:], XK[:, 2, :], start=True, stop=True), ("xv", 0))
            for b in range(B):
                ln_turn(1, b)
            for b in range(B):
                pe.wait_ge(sem("xt_ready"), B + b + 1)
                o = begin(("xq", b))
                done(pe.matmul(o, XK[:, 0, :], XT[:, b], start=True, stop=True), ("xq", b))
            pe.wait_ge(sem("xk_sb"), 1)
            for b in range(B):
                pe.wait_ge(sem("xq_sb"), b + 1)
                o = begin(("xs", b))
                done(pe.matmul(o[b * CK:(b + 1) * CK, :], xkT[:, b * CK:(b + 1) * CK], xqT[:, b],
                               start=True, stop=True), ("xs", b))
            pe.wait_ge(sem("xv_sb"), 1)
            for b in range(B):
                pe.wait_ge(sem("logits"), b + 1)
                o = begin(("xo", b))
                r = slice(b * CK, (b + 1) * CK)
                for t in range(QT):
                    mm = pe.matmul(o[:, t * P:(t + 1) * P], LT[r, b, t * P:(t + 1) * P], xv[r, :],
                                   start=True, stop=True)
                done(mm, ("xo", b))
            if stop > 2:
                for b in range(B):
                    ln_turn(2, b)
                tensor_c(pe, begin, done)
            if stop > 3:
                tensor_d(pe, begin, done, ln_turn)
            if stop > 4:
                tensor_e(pe, begin, done, ln_turn)
            if stop > 5:
                tensor_f(pe, begin, done)

        @block.scalar
        def _(act):
            def rstd(k, b, eps="eps_ln"):
                act.wait_ge(sem("ln_stats"), k * B + b + 1)
                act.activation(RSTD[:, b, 0], MV[:, b, :, 1], ACT.Ln, bias=const(eps)).then_inc(sem("ln_log"), 1)
                act.wait_ge(sem("ln_log"), k * B + b + 1)
                act.activation(RSTD[:, b, 1], RSTD[:, b, 0], ACT.Exp, scale=-0.5).then_inc(sem("ln_rstd"), 1)

            def xt_out(k, b):
                full(act, ("ln", k, b))
                act.copy(XT[:, b], bank(("ln", k, b))).then_inc(sem("xt_ready"), 1)

            def squares(u):
                p = u % PAIRS
                for hd, key in ((0, "QA"), (1, "QB")):
                    full(act, (key, u))
                    r = slice(64, 128) if hd == 0 else slice(0, 64)
                    c = 4 * (2 * p + hd)
                    act.activation(MQ[r, hd, :], bank((key, u))[r, :], ACT.Square,
                                   bias=BT0[r, c:c + 1]).then_inc(sem("mq_squared"), 1)

            def gates(u):
                full(act, ("G", u))
                if u >= 3:
                    act.wait_ge(sem("gr"), u - 2)
                p = u % PAIRS
                for hd in range(2):
                    r = slice(hd * 64, hd * 64 + 64)
                    c = 4 * (2 * p + hd) + 3
                    ins = act.activation(GA[r, u % 3, :], bank(("G", u))[r, :], ACT.Identity, bias=BT0[r, c:c + 1])
                ins.then_inc(sem("g_sb"), 1)

            def root(u, hd):
                act.wait_ge(sem("guarded"), 8 * u + 4 * hd + 4)
                d = D[:, u % 2, hd].rearrange("p k q -> p (k q)")
                act.activation(d, d, ACT.Sqrt).then_inc(sem("rooted"), 1)

            def weights(u):
                act.preload_act_table_set("natural_log_exp_and_others")
                for hd in range(2):
                    d = D[:, u % 2, hd].rearrange("p k q -> p (k q)")
                    act.wait_ge(sem("rooted"), 2 * u + hd + 1)
                    act.activation(d, d, ACT.Ln, bias=const("eps_w")).then_inc(sem("logged"), 1)
                for hd in range(2):
                    d = D[:, u % 2, hd].rearrange("p k q -> p (k q)")
                    act.wait_ge(sem("logged"), 2 * u + hd + 1)
                    act.activation(d, d, ACT.Exp, scale=-2.0).then_inc(sem("w_ready"), 1)

            def row_sums(u):
                full(act, ("RS", u))
                if u >= 1:
                    act.wait_ge(sem("rs_inv"), u)
                act.activation(LR, bank(("RS", u)), ACT.Ln, bias=const("eps_w")).then_inc(sem("rs_log"), 1)
                act.wait_ge(sem("rs_log"), u + 1)
                if u >= 1:
                    act.wait_ge(sem("gr"), u)
                act.activation(RR, LR, ACT.Exp, scale=-1.0).then_inc(sem("rs_inv"), 1)

            act.wait_ge(sem("consts_in"), 16)
            act.preload_act_table_set("natural_log_exp_and_others")
            for b in range(B):
                rstd(0, b)
            for b in range(B):
                xt_out(0, b)
            act.wait_ge(sem("bias_cols"), 2)
            squares(0)
            gates(0)
            for u in range(UNITS):
                root(u, 0)
                if u + 1 < UNITS:
                    squares(u + 1)
                    gates(u + 1)
                root(u, 1)
                weights(u)
                if u >= 1:
                    row_sums(u - 1)
            row_sums(UNITS - 1)

            full(act, ("xmask", 0))
            act.wait_ge(sem("h_done"), UNITS)
            act.copy(MT, bank(("xmask", 0))).then_inc(sem("mask_sb"), 1)
            full(act, ("ctxT", 0))
            act.copy(CTXT[:], bank(("ctxT", 0))[:, 0:P]).then_inc(sem("ctxT_sb"), 1)
            full(act, ("xk", 0))
            c = NCOL["L0_xattn_bias_k"]
            act.activation(xkT, bank(("xk", 0))[:, 0:P], ACT.Relu, bias=BN[:, c:c + 1]).then_inc(sem("xk_sb"), 1)
            for b in range(B):
                rstd(1, b)
            for b in range(B):
                xt_out(1, b)
            c = NCOL["L0_xattn_bias_q"]
            for b in range(B):
                full(act, ("xq", b))
                act.activation(xqT[:, b], bank(("xq", b)), ACT.Relu, bias=BN[:, c:c + 1]).then_inc(sem("xq_sb"), 1)
            for b in range(B):
                full(act, ("xs", b))
                r = slice(b * CK, (b + 1) * CK)
                act.activation(LT[r, b], bank(("xs", b))[r, :], ACT.Relu,
                               scale=float(1 / np.sqrt(P))).then_inc(sem("xs_relu"), 1)
            if stop > 2:
                for b in range(B):
                    rstd(2, b)
                for b in range(B):
                    xt_out(2, b)
                scalar_c(act)
            if stop > 3:
                scalar_d(act, rstd, xt_out)
            if stop > 4:
                scalar_e(act, rstd, xt_out)
            if stop > 5:
                scalar_f(act, rstd)

        @block.vector
        def _(dve):
            steps = [0]

            def link(ins):
                steps[0] += 1
                ins.then_inc(sem("dve_chain"), 1)
                dve.wait_ge(sem("dve_chain"), steps[0])

            def stats(k, b):
                if k:
                    dve.wait_ge(sem("x_new"), (k - 1) * B + b + 1)
                else:
                    dve.wait_ge(sem("x_in"), 16 * B)
                for t in range(QT):
                    ins = dve.bn_stats(STAT[:, b, t, :], X[:, b, t, :])
                link(ins)
                for t in range(QT):
                    ins = dve.bn_aggr(MV[:, b, t, :], STAT[:, b, t, :])
                ins.then_inc(sem("ln_stats"), 1)

            def normalize(k, b):
                dve.wait_ge(sem("ln_rstd"), k * B + b + 1)
                dve.wait_ge(sem("ln_stats"), k * B + b + 1)
                for t in range(QT):
                    ins = dve.tensor_scalar(Y[:, b, t, :], X[:, b, t, :], MV[:, b, t, 0:1],
                                            RSTD[:, b, 1, t:t + 1], ALU.subtract, ALU.mult)
                ins.then_inc(sem("ln_y"), 1)

            def layernorm(k):
                for b in range(B):
                    stats(k, b)
                    if b:
                        normalize(k, b - 1)
                normalize(k, B - 1)

            def evacuate(u):
                p = u % PAIRS
                for hd, key in ((0, "QA"), (1, "QB")):
                    full(dve, (key, u))
                    r = slice(hd * 64, hd * 64 + 64)
                    c = 4 * (2 * p + hd)
                    dve.tensor_scalar(MQ[r, hd, :], bank((key, u))[r, :], BT0[r, c:c + 1], -2.0,
                                      ALU.add, ALU.mult).then_inc(sem("mq_scaled"), 1)
                full(dve, ("K", u))
                for hd in range(2):
                    r = slice(hd * 64, hd * 64 + 64)
                    c = 4 * (2 * p + hd) + 1
                    dve.tensor_scalar(SK[r, hd, :], bank(("K", u))[r, :], BT0[r, c:c + 1], None,
                                      ALU.add).then_inc(sem("k_sb"), 1)
                full(dve, ("V", u))
                dve.tensor_tensor(VA[:, u % 3], bank(("V", u)).rearrange("p (k e) -> p k e", k=QT),
                                  BV[:, 2 * p:2 * p + 2, :].rearrange("p h e -> p (h e)").unsqueeze(1)
                                  .to_broadcast([P, QT, P]), ALU.add).then_inc(sem("v_sb"), 1)

            def key_norms(u):
                full(dve, ("k2", u))
                dve.tensor_copy(K2[:, u % 2], bank(("k2", u)).rearrange("p (k h e) -> p k h e", k=QT, h=2)[:, :, :, 0]
                                ).then_inc(sem("k2_sb"), 1)

            def guard(u, c):
                hd, kt = divmod(c, QT)
                if c == 0:
                    dve.wait_ge(sem("k2_sb"), u + 1)
                full(dve, ("S", u, c))
                dve.tensor_scalar(D[:, u % 2, hd, kt, :], bank(("S", u, c)), K2[:, u % 2, kt, hd:hd + 1], 1e-30,
                                  ALU.add, ALU.max).then_inc(sem("guarded"), 1)

            def gated(u):
                full(dve, ("PV", u))
                dve.wait_ge(sem("gr"), u + 1)
                b, p = divmod(u, PAIRS)
                dve.tensor_tensor(HT[:, b % 2, p, :], bank(("PV", u)), GR, ALU.mult).then_inc(sem("h_done"), 1)

            def add_to_stream(k, b, key):
                full(dve, key)
                dve.tensor_tensor(X[:, b], X[:, b], bank(key).rearrange("p (t d) -> p t d", t=QT),
                                  ALU.add).then_inc(sem("x_new"), 1)

            dve.wait_ge(sem("consts_in"), 16)
            dve.tensor_copy(identb[:], ident).then_inc(sem("identb_ready"), 1)
            full(dve, ("tb", 0))
            dve.tensor_copy(BT0[:], bank(("tb", 0))[:, 0:64]).then_inc(sem("bias_cols"), 1)
            full(dve, ("tb", 1))
            dve.tensor_copy(BN[:, 0:38], bank(("tb", 1))[:, 0:38]).then_inc(sem("bias_cols"), 1)
            dve.memset(SK[64:128, 0, :], 1.0)
            dve.memset(SK[0:64, 1, :], 1.0)
            layernorm(0)
            dve.wait_ge(sem("bias_cols"), 2)
            dve.wait_ge(sem("bcast_in"), 48)
            evacuate(0)
            key_norms(0)
            for u in range(UNITS):
                for c in range(4):
                    if c == 0 and u >= 2:
                        full(dve, ("RS", u - 2))
                    guard(u, c)
                if u >= 2:
                    gated(u - 2)
                for c in range(4, 8):
                    guard(u, c)
                if u + 1 < UNITS:
                    evacuate(u + 1)
                    key_norms(u + 1)
                if u >= 2 and (u - 2) % PAIRS == PAIRS - 1:
                    b = (u - 2) // PAIRS
                    if b == 0:
                        dve.wait_ge(sem("x_biased"), B)
                    add_to_stream(0, b, ("out0", b))
            gated(UNITS - 2)
            gated(UNITS - 1)
            add_to_stream(0, B - 1, ("out0", B - 1))

            layernorm(1)
            full(dve, ("xv", 0))
            dve.tensor_tensor(xtmp, bank(("xv", 0))[:, 0:P], BXV[:], ALU.add).then_inc(sem("xv_sum"), 1)
            dve.wait_ge(sem("xv_sum"), 1)
            dve.tensor_scalar(xv, xtmp, 0.0, None, ALU.max).then_inc(sem("xv_sb"), 1)
            dve.wait_ge(sem("mask_sb"), 1)
            for b in range(B):
                r = slice(b * CK, (b + 1) * CK)
                dve.wait_ge(sem("xs_relu"), b + 1)
                dve.tensor_tensor(LT[r, b], LT[r, b], MT[r, :], ALU.add).then_inc(sem("logits"), 1)
            for b in range(B):
                full(dve, ("xo", b))
                dve.scalar_tensor_tensor(out=X[:, b], in0=bank(("xo", b)).rearrange("p (t d) -> p t d", t=QT),
                                         scalar=0.0, in1=X[:, b], op0=ALU.max, op1=ALU.add
                                         ).then_inc(sem("x_new"), 1)
            if stop > 2:
                layernorm(2)
                vector_c(dve, link)
            if stop > 3:
                vector_d(dve, link, layernorm, add_to_stream)
            if stop > 4:
                vector_e(dve, link, layernorm, add_to_stream)
            if stop > 5:
                vector_f(dve, link, stats, normalize)

        @block.gpsimd
        def _(pool):
            pool.memset(QKROW[:], 0.0).then_inc(sem("row_set"), 1)
            pool.wait_ge(sem("row_set"), 1)
            pool.memset(QKROW[:, GROUPS:].rearrange("o g (j r) -> o (g j) r", r=32)[:, :, 24:27], 1.0
                        ).then_inc(sem("row_set"), 1)

            def key_squares(u):
                for hd in range(2):
                    r = slice(hd * 64, hd * 64 + 64)
                    pool.wait_ge(sem("k_sb"), 2 * u + hd + 1)
                    pool.tensor_tensor(KSQ[r, :], SK[r, hd, :], SK[r, hd, :], ALU.mult).then_inc(sem("ksq"), 1)
                    pool.wait_ge(sem("ksq"), 2 * u + hd + 1)

            def scale_gates(u):
                pool.wait_ge(sem("rs_inv"), u + 1)
                pool.wait_ge(sem("g_sb"), u + 1)
                if u >= 1:
                    pool.wait_ge(sem("h_done"), u)
                pool.tensor_tensor(GR, GA[:, u % 3, :], RR, ALU.mult).then_inc(sem("gr"), 1)
                pool.wait_ge(sem("gr"), u + 1)

            key_squares(0)
            pool.wait_ge(sem("bcast_in"), 48)
            for b in range(B):
                pool.wait_ge(sem("ln_y"), b + 1)
                pool.tensor_tensor(X[:, b], X[:, b], Bout[:].unsqueeze(1).to_broadcast([P, QT, P]),
                                   ALU.add).then_inc(sem("x_biased"), 1)
            pool.wait_ge(sem("x_biased"), B)
            for u in range(UNITS):
                if u + 1 < UNITS:
                    key_squares(u + 1)
                if u >= 1:
                    scale_gates(u - 1)
            scale_gates(UNITS - 1)
            if stop > 2:
                pool_c(pool)
            if stop > 4:
                pool_e(pool)


def kernel(**inputs):
    import numpy as _np
    import concourse.bacc as _bacc
    from concourse import mybir as _mybir
    from concourse.bass_utils import run_bass_kernel_spmd as _run

    nc = _bacc.Bacc("TRN2", target_bir_lowering=False, num_devices=1)
    given = dict(inputs)
    given["consts"] = _np.concatenate([c.astype(_np.float32) for c in constant_columns().values()], axis=1)
    given["window_bias"] = window_bias()
    arrays, aps = {}, {}
    for name, value in given.items():
        v = _np.ascontiguousarray(value)
        arrays[f"in_{name}_dram"] = v
        aps[name] = nc.dram_tensor(f"in_{name}_dram", v.shape, _mybir.dt.from_np(v.dtype), kind="ExternalInput").ap()
    result = nc.dram_tensor("out_0_dram", (B, S, P), _mybir.dt.float32, kind="ExternalOutput").ap()
    decoder_kernel(nc, aps, result)
    r = _run(nc, [arrays], core_ids=[0])
    return r.results[0]["out_0_dram"]
```
